# Optimizing a Trainium2 kernel written in Bass

```python
import numpy as np
import jax
import jax.numpy as jnp

def _softmax(x, axis=-1):
    return jax.nn.softmax(x, axis=axis)

def _gelu(x):
    return jax.nn.gelu(x, approximate=True)

def _silu(x):
    return jax.nn.silu(x)

def _sigmoid(x):
    return jax.nn.sigmoid(x)

def _layernorm(x, axis=-1, eps=1e-05):
    m = jnp.mean(x, axis=axis, keepdims=True)
    v = jnp.var(x, axis=axis, keepdims=True)
    return (x - m) / jnp.sqrt(v + eps)

def _scatter_add(tgt, idx, src, axis=0):
    return tgt.at[idx].add(src)

def _segment_sum(src, seg, n):
    return jax.ops.segment_sum(src, seg, n)
kernel_name = 'mk_adaln_d1_jaxref_r8_aa772b'

def setup_inputs(seed: int=0):
    np.random.seed(seed)
    _w = jnp.asarray

    def _L0_attn_setup():
        import jax, jax.numpy as jnp
        import numpy as np
        EMBED_DIM = 128
        NUM_HEADS = 16
        HEAD_DIM = EMBED_DIM // NUM_HEADS
        LAMBDA_ENTANGLE = 0.35
        key = jax.random.key(seed)
        ks = jax.random.split(key, 10)
        B, S, D = (2, 256, EMBED_DIM)
        init = 1.0 / np.sqrt(D)
        x = jax.random.normal(ks[0], (B, S, D), dtype=jnp.float32)
        Wq = jax.random.uniform(ks[1], (D, D), jnp.float32, -init, init)
        bq = jax.random.uniform(ks[2], (D,), jnp.float32, -init, init)
        Wk = jax.random.uniform(ks[3], (D, D), jnp.float32, -init, init)
        bk = jax.random.uniform(ks[4], (D,), jnp.float32, -init, init)
        Wv = jax.random.uniform(ks[5], (D, D), jnp.float32, -init, init)
        bv = jax.random.uniform(ks[6], (D,), jnp.float32, -init, init)
        Wo = jax.random.uniform(ks[7], (D, D), jnp.float32, -init, init)
        bo = jax.random.uniform(ks[8], (D,), jnp.float32, -init, init)
        J_attn = jax.random.normal(ks[9], (NUM_HEADS, HEAD_DIM, HEAD_DIM), dtype=jnp.float32) * 0.02
        lambda_attn = jnp.asarray(LAMBDA_ENTANGLE, dtype=jnp.float32)
        return {'x': x, 'Wq': Wq, 'bq': bq, 'Wk': Wk, 'bk': bk, 'Wv': Wv, 'bv': bv, 'Wo': Wo, 'bo': bo, 'J_attn': J_attn, 'lambda_attn': lambda_attn}
    _L0_attn_in = _L0_attn_setup()

    def _L0_ffn_setup():
        import jax, jax.numpy as jnp
        import numpy as np
        B, S, D, F, E = (1, 128, 128, 512, 8)
        EPS = 1e-05

        def _sublayer(xs, g, b, W1e, b1e, W2e, b2e):
            mu = jnp.mean(xs, axis=-1, keepdims=True)
            var = jnp.mean(jnp.square(xs - mu), axis=-1, keepdims=True)
            h = (xs - mu) * jax.lax.rsqrt(var + EPS) * g + b
            return xs + jax.nn.relu(h @ W1e.T + b1e) @ W2e.T + b2e
        key = jax.random.key(seed)
        ks = jax.random.split(key, 4)
        x = jax.random.normal(ks[0], (B, S, D), jnp.float32)
        centroids = jax.random.normal(ks[1], (E, D), jnp.float32) * 0.1
        gamma = jnp.ones((E, D), jnp.float32)
        beta = jnp.zeros((E, D), jnp.float32)
        W1 = jax.random.normal(ks[2], (E, F, D), jnp.float32) * 0.02
        b1 = jnp.zeros((E, F), jnp.float32)
        W2 = jax.random.normal(ks[3], (E, D, F), jnp.float32) * 0.02
        b2 = jnp.zeros((E, D), jnp.float32)
        return {'x': x, 'centroids': centroids, 'gamma': gamma, 'beta': beta, 'W1': W1, 'b1': b1, 'W2': W2, 'b2': b2}
    _L0_ffn_in = _L0_ffn_setup()
    _L0_c = _w((lambda *s: np.random.randn(*s).astype(np.float32) * 0.05)(4, 128))
    _L0_wmod = _w((lambda *s: np.random.randn(*s).astype(np.float32) * 0.05)(128, 6 * 128) * 128 ** (-0.5))
    _d = {'L0_attn_x': _L0_attn_in['x'], 'L0_attn_Wq': _L0_attn_in['Wq'], 'L0_attn_bq': _L0_attn_in['bq'], 'L0_attn_Wk': _L0_attn_in['Wk'], 'L0_attn_bk': _L0_attn_in['bk'], 'L0_attn_Wv': _L0_attn_in['Wv'], 'L0_attn_bv': _L0_attn_in['bv'], 'L0_attn_Wo': _L0_attn_in['Wo'], 'L0_attn_bo': _L0_attn_in['bo'], 'L0_attn_J_attn': _L0_attn_in['J_attn'], 'L0_attn_lambda_attn': _L0_attn_in['lambda_attn'], 'L0_ffn_centroids': _L0_ffn_in['centroids'], 'L0_ffn_gamma': _L0_ffn_in['gamma'], 'L0_ffn_beta': _L0_ffn_in['beta'], 'L0_ffn_W1': _L0_ffn_in['W1'], 'L0_ffn_b1': _L0_ffn_in['b1'], 'L0_ffn_W2': _L0_ffn_in['W2'], 'L0_ffn_b2': _L0_ffn_in['b2'], 'L0_c': _L0_c, 'L0_wmod': _L0_wmod}
    _x0 = _d['L0_attn_x']
    _d['L0_attn_x'] = jax.random.normal(jax.random.fold_in(jax.random.key(seed), 1), (4, 1024, 128), dtype=_x0.dtype)
    del _x0
    return _d

def reference(L0_attn_x, L0_attn_Wq, L0_attn_bq, L0_attn_Wk, L0_attn_bk, L0_attn_Wv, L0_attn_bv, L0_attn_Wo, L0_attn_bo, L0_attn_J_attn, L0_attn_lambda_attn, L0_ffn_centroids, L0_ffn_gamma, L0_ffn_beta, L0_ffn_W1, L0_ffn_b1, L0_ffn_W2, L0_ffn_b2, L0_c, L0_wmod):

    def _L0_attn_ref(x, Wq, bq, Wk, bk, Wv, bv, Wo, bo, J_attn, lambda_attn):
        import jax, jax.numpy as jnp
        import numpy as np
        EMBED_DIM = 128
        NUM_HEADS = 16
        HEAD_DIM = EMBED_DIM // NUM_HEADS
        LAMBDA_ENTANGLE = 0.35
        B, S, D = x.shape
        H, Hd = (NUM_HEADS, HEAD_DIM)
        scale = jnp.sqrt(jnp.asarray(Hd, dtype=x.dtype))

        def heads(W, b):
            y = jnp.einsum('bsd,ed->bse', x, W) + b
            return y.reshape(B, S, H, Hd).transpose(0, 2, 1, 3)
        Q = heads(Wq, bq)
        K = heads(Wk, bk)
        V = heads(Wv, bv)
        scores = jnp.einsum('bhid,bhjd->bhij', Q, K) / scale
        QJ = jnp.einsum('bhid,hde->bhie', jnp.tanh(Q), J_attn)
        delta = jnp.einsum('bhie,bhje->bhij', QJ, jnp.tanh(K))
        scores = scores + lambda_attn * delta
        causal = jnp.triu(jnp.ones((S, S), dtype=bool), k=1)
        scores = jnp.where(causal, -jnp.inf, scores)
        probs = jax.nn.softmax(scores, axis=-1)
        out = jnp.einsum('bhij,bhjd->bhid', probs, V)
        out = out.transpose(0, 2, 1, 3).reshape(B, S, D)
        return jnp.einsum('bsd,ed->bse', out, Wo) + bo

    def _L0_ffn_ref(x, centroids, gamma, beta, W1, b1, W2, b2):
        import jax, jax.numpy as jnp
        import numpy as np
        B, S, D, F, E = (1, 128, 128, 512, 8)
        EPS = 1e-05

        def _sublayer(xs, g, b, W1e, b1e, W2e, b2e):
            mu = jnp.mean(xs, axis=-1, keepdims=True)
            var = jnp.mean(jnp.square(xs - mu), axis=-1, keepdims=True)
            h = (xs - mu) * jax.lax.rsqrt(var + EPS) * g + b
            return xs + jax.nn.relu(h @ W1e.T + b1e) @ W2e.T + b2e
        feats = x.reshape(-1, x.shape[-1])
        scores = jax.lax.stop_gradient(feats @ centroids.T)
        expert = jnp.argmax(scores, axis=1)
        onehot = jax.nn.one_hot(expert, E, dtype=feats.dtype)
        alpha = jax.nn.sigmoid(jnp.sum(feats * centroids[expert], axis=-1, keepdims=True))
        ys = jax.vmap(_sublayer, in_axes=(None, 0, 0, 0, 0, 0, 0))(feats, gamma, beta, W1, b1, W2, b2)
        y = jnp.einsum('te,etd->td', onehot, ys)
        out = alpha * y + (1.0 - alpha) * feats
        return out.reshape(x.shape)
    x = L0_attn_x
    mod = (_silu(L0_c) @ L0_wmod).reshape(L0_c.shape[0], 6, 1, -1)
    sa, ca, ga, sb, cb, gb = (mod[:, 0], mod[:, 1], mod[:, 2], mod[:, 3], mod[:, 4], mod[:, 5])
    ga = (2 * (ga >= 0) - 1) * jnp.maximum(jnp.abs(ga), 0.25)
    gb = (2 * (gb >= 0) - 1) * jnp.maximum(jnp.abs(gb), 0.25)
    h = _layernorm(x, axis=-1) * (1 + ca) + sa
    x = x + ga * _L0_attn_ref(h, L0_attn_Wq, L0_attn_bq, L0_attn_Wk, L0_attn_bk, L0_attn_Wv, L0_attn_bv, L0_attn_Wo, L0_attn_bo, L0_attn_J_attn, L0_attn_lambda_attn)
    h = _layernorm(x, axis=-1) * (1 + cb) + sb
    x = x + gb * _L0_ffn_ref(h, L0_ffn_centroids, L0_ffn_gamma, L0_ffn_beta, L0_ffn_W1, L0_ffn_b1, L0_ffn_W2, L0_ffn_b2)
    return x

_drawn_inputs = setup_inputs


def setup_inputs(seed=0):
    import zlib

    import numpy as np

    out = dict(_drawn_inputs(seed))
    spreads = {'L0_ffn_gamma': (1.0, 0.6),
     'L0_ffn_beta': (0.0, 0.8),
     'L0_ffn_b1': (0.0, 0.8),
     'L0_ffn_b2': (0.0, 1.177)}
    factors = {'L0_attn_Wq': 8.0,
     'L0_attn_bq': 8.0,
     'L0_attn_Wk': 8.0,
     'L0_attn_bk': 29.073,
     'L0_attn_Wv': 7.113,
     'L0_attn_bv': 6.932,
     'L0_attn_Wo': 5.117,
     'L0_attn_bo': 4.225,
     'L0_attn_J_attn': 8.0,
     'L0_ffn_W1': 4.365,
     'L0_ffn_W2': 3.381}
    for name, (base, spread) in spreads.items():
        noise = np.random.default_rng([zlib.crc32(name.encode()), seed]).standard_normal(out[name].shape)
        drawn = base * np.exp(spread * noise) if base else spread * noise
        out[name] = jnp.asarray(drawn.astype(out[name].dtype))
    for name, factor in factors.items():
        out[name] = (out[name] * factor).astype(out[name].dtype)
    return out
```

```python
import concourse.bass as bass
from concourse import mybir
from contextlib import ExitStack

F32 = mybir.dt.float32
BF16 = mybir.dt.bfloat16
I32 = mybir.dt.int32
ALU = mybir.AluOpType
ACT = mybir.ActivationFunctionType
AX = mybir.AxisListType

B, S, D = 4, 1024, 128
H, HD = 16, 8
E, FF = 8, 512
P = 128
TB = S // P
NT = B * TB
HG = 4
NG = H // HG
GROUPS = B * NG
HALF = 512
EPS = 1e-5
BIG = 1e30
FC = FF // P
SLOT_TILES = (B * S + E * (P - 1)) // P + 1
assert SLOT_TILES == 40
ROW = 2 * HD
TERMS = 6
KROWS = ROW * TERMS
MROWS = KROWS + 3
VW = HD + 1


def build(nc, x, Wq, bq, Wk, bk, Wv, bv, Wo, bo, J, lam, cent, gamma, beta, W1, b1, W2, b2, c, wmod, out):
    ctx = ExitStack()
    with ctx:
        def sb(name, shape, dt=F32):
            return ctx.enter_context(nc.sbuf_tensor(name, shape, dt))

        def sem(name):
            return ctx.enter_context(nc.semaphore(name))

        def dram(name, shape, dt=F32):
            return nc.dram_tensor(name, shape, dt, kind="Internal").ap()

        q_parts = dram("q_parts", [B, H, 3, ROW, S], BF16)
        k_parts = dram("k_parts", [B, H, 3, ROW, S], BF16)
        v_aug = dram("v_aug", [B, NG, P, TB, HG * VW])
        o_raw = dram("o_raw", [B, NG, P, S])
        x_sorted = dram("x_sorted", [SLOT_TILES * P, D])
        y_sorted = dram("y_sorted", [SLOT_TILES * P, D])

        X = sb("X", [P, NT, D])
        ident = sb("ident", [P, P])
        identb = sb("identb", [P, P], BF16)
        mask = sb("mask", [P, S])
        wT = sb("wT", [P, 4, D])
        rows = sb("rows", [64, D])
        cols = sb("cols", [P, 64])
        JB = sb("JB", [P, P])
        JL = sb("JL", [P, P])
        lam_c = sb("lam_c", [P, 1])
        bqs = sb("bqs", [P, 1])
        bv_b = sb("bv_b", [P, D])
        bo_b = sb("bo_b", [P, D])
        silu = sb("silu", [P, 4, B])
        modT = sb("modT", [P, 2, B])
        MB = sb("MB", [P, B, 4, D])
        gtmp = sb("gtmp", [P, 2, B, D])
        stat = sb("stat", [P, NT, 6])
        lnt = sb("lnt", [P, 12, NT])
        maxima = sb("maxima", [P, 4, HG * TB])
        mres = sb("mres", [P, 2, HG * TB])
        mparts = sb("mparts", [P, HG, 3, TB], BF16)
        mrow = sb("mrow", [HG * 3 * TB, P], BF16)
        XN = sb("XN", [P, TB, D])
        HT = sb("HT", [P, S])
        OT = XN[:, :, :].rearrange("p t d -> p (t d)").rearrange("p (a q) -> p a q", a=2)
        Vs = sb("Vs", [P, 4, TB * HG * VW])
        b2_b = sb("b2_b", [P, E * D])
        arenaA = sb("arenaA", [P, 24576])
        arenaB = sb("arenaB", [P, 12544])
        Aap = arenaA[:, :]
        Bap = arenaB[:, :]
        stacks = Aap[:, 0:16384].bitcast(BF16).rearrange("p (r s h q) -> p r s h q", r=4, s=2, h=HG)
        SQ = lambda r, h: stacks[:, r, 0, h, :]
        SK = lambda r, h: stacks[:, r, 1, h, :]
        PT = Aap[:, 16384:24576].rearrange("p (r h q) -> p r h q", r=4, h=HG)
        wraw = Aap[:, 16384:16896].rearrange("p (n d) -> p n d", n=4)
        silu_b = Aap[:, 16896:17408].rearrange("p (b d) -> p b d", b=B)
        wm = Aap[:, 17408:18176]
        NUM = Aap[:, 0:4096]
        DEN = Aap[:, 4096:8192]
        H2 = Aap[:, 0:4096].rearrange("p (t d) -> p t d", d=D)
        XH = Aap[:, 4096:8192].rearrange("p (t d) -> p t d", d=D)
        YG = Aap[:, 8192:12288].rearrange("p (t d) -> p t d", d=D)
        AT = Aap[:, 12288:16384]
        W1r = Aap[:, 16384:20480].rearrange("p (k d) -> p k d", d=D)
        W2r = Aap[:, 20480:24576].rearrange("p (k d) -> p k d", d=D)
        T32 = Bap[:, 0:5120].rearrange("p (k s) -> p k s", k=5)
        T16 = Bap[:, 5120:11264].bitcast(BF16).rearrange("p (k j s) -> p k j s", k=4, j=3)
        VA = Bap[:, 11264:11264 + TB * H * VW].rearrange("p (t h w) -> p t h w", t=TB, h=H)
        W1T = Bap[:, 0:4096]
        W2T = Bap[:, 4096:8192]
        FB = 8192
        XS = Bap[:, FB:FB + 512].rearrange("p (r d) -> p r d", r=4)
        XT = Bap[:, FB + 512:FB + 768].rearrange("p (r d) -> p r d", r=2)
        HS = Bap[:, FB + 768:FB + 1792].rearrange("p (r d) -> p r d", r=2)
        HR = Bap[:, FB + 1792:FB + 2816].rearrange("p (r d) -> p r d", r=2)
        YS = Bap[:, FB + 2816:FB + 3072].rearrange("p (r d) -> p r d", r=2)
        WOG = sb("WOG", [P, B, D])
        triu = sb("triu", [P, P], BF16)
        onesb = sb("onesb", [P, P], BF16)
        after = sb("after", [P, P], BF16)
        iota_e = sb("iota_e", [P, E])
        iota_t = sb("iota_t", [P, SLOT_TILES])
        iota_n = sb("iota_n", [P, NT])
        iotai = sb("iotai", [P, 96], I32)
        sc = Aap[:, 18432:18688].rearrange("p (t e) -> p t e", e=E)
        rt = Aap[:, 16384:18432].rearrange("p (k t e) -> p k t e", k=8, e=E)
        rs = Aap[:, 18688:19008].rearrange("p (k t) -> p k t", k=8)
        ohb = sb("ohb", [P, NT * E], BF16)
        slot = sb("slot", [P, NT], I32)
        tile_e = sb("tile_e", [P, SLOT_TILES], I32)
        zero = Aap[:, 18176:18176 + SLOT_TILES * D // 8]
        PS = ctx.enter_context(nc.psum_tensor("PS", [P, 8, HALF], F32))

        ps2 = lambda k: PS[:, k:k + 2, :].rearrange("p a b -> p (a b)")

        (x_in, w_in, rows_in, bias_in, j_in, consts_ok, pool_chain, dve_chain, cols_ps, cols_ok, silu_e, silu_ok,
         mod_ps, mod_ok, wT_ps, wT_ok, stats_ok, root_ok, xn_ok, xt_ps, ht_ok, q_ps, tanh_ok, k_ps, v_ps,
         qj_ps, first_ok, split_step, split_ok, va_ok, parts_out, v_out, max_ps, max_used, m_split,
         m_parts_ok, m_in, s_ps, exp_ok, pv_ok, ot_ok, num_in, at_ok, o_ps, x1_ok, w12_in, w_tr, w_ev,
         h2_ok, h2t_ps, h2t_ok, score_ps, alpha_e, oh_ok, cnt_ps, slots_ok, zero_out, sorted_out, xsT_ps,
         xt_ok, h_ps, hs_ok, hT_ps, hr_ok, y_ps, ys_ok, fin_ok, out_done, res_ok, bn_ok, max_seen) = [sem(n) for n in (
            "x_in w_in rows_in bias_in j_in consts_ok pool_chain dve_chain cols_ps cols_ok silu_e silu_ok mod_ps "
            "mod_ok wT_ps wT_ok stats_ok root_ok xn_ok xt_ps ht_ok q_ps tanh_ok k_ps v_ps qj_ps first_ok "
            "split_step split_ok va_ok parts_out v_out max_ps max_used m_split m_parts_ok m_in s_ps exp_ok "
            "pv_ok ot_ok num_in at_ok o_ps x1_ok w12_in w_tr w_ev h2_ok h2t_ps h2t_ok score_ps alpha_e oh_ok "
            "cnt_ps slots_ok zero_out sorted_out xsT_ps xt_ok h_ps hs_ok hT_ps hr_ok y_ps ys_ok fin_ok out_done "
            "res_ok bn_ok max_seen").split()]

        stack_in = [sem(f"stack_in{g}") for g in range(NG)]
        ot_out = [sem(f"ot_out{k}") for k in range(2)]
        xs_in = [sem(f"xs_in{k}") for k in range(4)]
        y_out = [sem(f"y_out{k}") for k in range(2)]
        gathered = [sem(f"gathered{b}") for b in range(B)]

        block = ctx.enter_context(nc.Block())

        UNITS = [(qc, kb) for qc in range(2) for kb in range(4 * qc + 4)]
        NU = len(UNITS)
        DIAG = [u for u, (qc, kb) in enumerate(UNITS) if kb >= 4 * qc]
        HALF_END = {max(u for u, (qc, _) in enumerate(UNITS) if qc == q): q for q in range(2)}
        LAG = 2
        SB_, EB, MB_ = 3, 4, 2
        MTILES = [(h, t) for h in range(HG) for t in range(TB)]
        NM = len(MTILES)
        EARLY = 8
        SEQ = [("m", 1, k) for k in range(EARLY, NM)] + [("m", 2, 0), ("m", 2, 1), ("T", 1, 0)] + \
              [("m", 2, k) for k in range(2, EARLY)]
        FIRST = [("m", 0, k) for k in range(NM)] + [("m", 1, 0), ("m", 1, 1), ("T", 0, 0)] + \
                [("m", 1, k) for k in range(2, EARLY)]
        PER = len(SEQ)
        cost = [MTILES[k][1] + 1 if kind == "m" else 1 for kind, _, k in SEQ]
        STEP = [min(NU - 1, int((sum(cost[:i]) + cost[i] / 2) * NU / sum(cost))) for i in range(PER)]
        T_AT = SEQ.index(("T", 1, 0))
        T_FIRST = FIRST.index(("T", 0, 0))

        def items(g, b_last):
            for i, (kind, ahead, k) in enumerate(SEQ):
                if not b_last or g + ahead < NG:
                    yield i, STEP[i], kind, (g + ahead) % NG, ahead, k

        def use(b, g, i):
            return (b * NG + g) * PER + i + len(FIRST)

        def left_out(g, i):
            return sum(g2 + ahead >= NG for g2 in range(g + 1) for j, (_, ahead, _) in enumerate(SEQ)
                       if g2 < g or j < i)

        assert (NG * PER) % MB_ == 0 and (NU * HG) % SB_ == 0 and NU % EB == 0

        @block.sync
        def _(sp):
            sp.dma_start(X[:, :, :], x.rearrange("b (t p) d -> p (b t) d", p=P)).then_inc(x_in, 16)
            sp.dma_start(wm[:, :], wmod).then_inc(w_in, 16)
            for n, w in enumerate((Wq, Wk, Wv, Wo)):
                sp.dma_start(wraw[:, n, :], w).then_inc(w_in, 16)
            sp.wait_ge(pool_chain, 1)
            for h in range(H):
                sp.dma_start(JB[h * HD:(h + 1) * HD, h * HD:(h + 1) * HD], J[h]).then_inc(j_in, 16)
            with sp.Fori(0, B) as b:
                for k, (dst, off) in enumerate(((q_parts, 0), (k_parts, 0), (k_parts, HD), (q_parts, HD))):
                    sp.wait_ge(split_ok, b * 4 + k + 1)
                    for j in range(3):
                        sp.dma_start(dst[bass.ds(b, 1), :, j, off:off + HD, :].rearrange("a h r q -> (a h) r q"),
                                     T16[:, k, j, :]).then_inc(parts_out, 16)
                sp.wait_ge(va_ok, b + 1)
                for g in range(NG):
                    sp.dma_start(v_aug[bass.ds(b, 1), g, :, :, :].rearrange("a p t w -> (a p) t w"),
                                 VA[:, :, HG * g:HG * g + HG, :].rearrange("p t h w -> p t (h w)")).then_inc(v_out, 16)
            sp.wait_ge(parts_out, B * 12 * 16)
            sp.wait_ge(v_out, B * NG * 16)

            Q_ROWS = ((0, 0, 3), (3, 0, 2), (5, 0, 1))
            K_ROWS = ((0, 0, 1), (1, 0, 1), (2, 0, 1), (3, 1, 1), (4, 1, 1), (5, 2, 1))

            def load_group(b, g):
                for side, src, terms in ((0, q_parts, Q_ROWS), (1, k_parts, K_ROWS)):
                    for t, j, n in terms:
                        sp.dma_start(stacks[t * ROW:(t + n) * ROW, g, side, :, :],
                                     src[bass.ds(b, 1), g * HG:(g + 1) * HG, j:j + n, :, :].rearrange("a h j r q -> (a j r) h q"))\
                            .then_inc(stack_in[g], 16)
                sp.dma_start(Vs[:, g, :], v_aug[bass.ds(b, 1), g, :, :, :].rearrange("a p t w -> (a p) (t w)"))\
                    .then_inc(stack_in[g], 16)

            def send_maxima(g, index):
                sp.wait_ge(max_used, index + 1 + MB_)
                for h in range(HG):
                    sp.dma_start(stacks[KROWS:MROWS, g, 0, h, :].rearrange("r (t q) -> r t q", t=TB),
                                 mrow[h * 3 * TB:(h + 1) * 3 * TB, :]).then_inc(m_in, 16)

            def store_half(b, g, half):
                sp.wait_ge(ot_ok, (b * NG + g) * 2 + half + 2)
                sp.dma_start(o_raw[bass.ds(b, 1), g, :, half * HALF:(half + 1) * HALF].rearrange("a p q -> (a p) q"),
                             OT[:, half, :]).then_inc(ot_out[half], 16)

            for g in range(NG):
                load_group(0, g)
            send_maxima(0, T_FIRST)

            def attention(b, last):
                for g in range(NG):
                    store_half(b, g, 0)
                    if not last or g + 1 < NG:
                        send_maxima((g + 1) % NG, use(b, g, T_AT) - (left_out(g, T_AT) if last else 0))
                    store_half(b, g, 1)
                    if not last:
                        sp.wait_ge(pv_ok, (b * NG + g + 1) * NU + EB)
                        load_group(b + 1, g)
            with sp.Fori(0, B - 1) as b:
                attention(b, False)
            attention(B - 1, True)

            for half in range(2):
                sp.wait_ge(ot_out[half], (GROUPS + 1) * 16)
            sp.wait_ge(pv_ok, GROUPS * NU + EB)
            for b in range(B):
                o_b = o_raw[b].rearrange("g (h r) q -> (g h) r q", h=HG)
                sp.dma_start(NUM[:, b * S:(b + 1) * S], o_b[:, 0:HD, :]).then_inc(num_in, 16)
                sp.dma_start(DEN[:, b * S:(b + 1) * S], o_b[:, HD:VW, :].to_broadcast([H, HD, S])).then_inc(num_in, 16)
            sp.dma_start(W1r, W1.rearrange("e (c f) d -> f (e c) d", f=P)).then_inc(w12_in, 16)
            sp.dma_start(W2r.rearrange("p (e c) f -> p e (c f)", e=E), W2.rearrange("e d n -> d e n")).then_inc(w12_in, 16)

            sp.wait_ge(sorted_out, NT * 16)
            with sp.Fori(0, SLOT_TILES // 4) as i:
                for j in range(4):
                    sp.wait_ge(xsT_ps, i * 4 + j + 1)
                    sp.dma_start(XS[:, j, :], x_sorted[bass.ds((i * 4 + j) * P, P), :]).then_inc(xs_in[j], 16)
            for b in range(B):
                sp.wait_ge(fin_ok, b + 1)
                sp.dma_start(out[b].rearrange("(t p) d -> p t d", p=P), YG[:, b * TB:(b + 1) * TB, :]).then_inc(out_done, 16)
            sp.wait_ge(out_done, B * 16)

        @block.gpsimd
        def _(pool):
            g = nc.gpsimd
            g.memset(ident[:, :], 0.0)
            g.memset(mask[:, :], 0.0)
            g.memset(triu[:, :], 1.0)
            g.memset(onesb[:, :], 1.0)
            g.memset(after[:, :], 0.0)
            g.memset(JB[:, :], 0.0)
            g.iota(iotai[:, 0:SLOT_TILES], [[1, SLOT_TILES]], base=0, channel_multiplier=0)
            g.iota(iotai[:, 48:48 + NT], [[P, NT]], base=0, channel_multiplier=0).then_inc(pool_chain, 1)
            pool.wait_ge(pool_chain, 1)
            g.affine_select(out=ident[:, :], in_=ident[:, :], compare_op=ALU.not_equal, fill=1.0, base=0,
                            pattern=[[-1, P]], channel_multiplier=1)
            g.affine_select(out=mask[:, S - P:S], in_=mask[:, S - P:S], compare_op=ALU.is_ge, fill=-BIG, base=0,
                            pattern=[[-1, P]], channel_multiplier=1)
            g.affine_select(out=after[:, :], in_=after[:, :], compare_op=ALU.is_ge, fill=-BIG, base=0,
                            pattern=[[1, P]], channel_multiplier=-1)
            g.affine_select(out=triu[:, :], in_=triu[:, :], compare_op=ALU.is_gt, fill=0.0, base=0,
                            pattern=[[1, P]], channel_multiplier=-1).then_inc(pool_chain, 1)
            pool.wait_ge(pool_chain, 2)
            g.tensor_copy(iota_e[:, :], iotai[:, 0:E])
            g.tensor_copy(iota_t[:, :], iotai[:, 0:SLOT_TILES])
            g.tensor_copy(iota_n[:, :], iotai[:, 48:48 + NT])
            g.memset(zero[:, :], 0.0)
            g.memset(VA[:, :, :, HD:VW], 1.0).then_inc(pool_chain, 1)
            for r in range(NG):
                pool.wait_ge(pool_chain, 3 + r)
                g.memset(stacks[KROWS:MROWS, r, 1, :, :], 1.0).then_inc(pool_chain, 1)
            pool.wait_ge(pool_chain, 3 + NG)
            g.tensor_copy(identb[:, :], ident[:, :]).then_inc(consts_ok, 1)
            pool.wait_ge(consts_ok, 1)
            for k in range(8):
                pool.dma_start(x_sorted.rearrange("(k p t) d -> k p (t d)", k=8, p=P)[k], zero[:, :]).then_inc(zero_out, 16)

            with pool.Fori(0, B) as b:
                for k in range(4):
                    pool.wait_ge(first_ok, b * 4 + k + 1)
                    a = T32[:, k, :]
                    g.tensor_tensor(a, a, T16[:, k, 0, :], ALU.subtract).then_inc(split_step, 1)
                    pool.wait_ge(split_step, b * 8 + 2 * k + 1)
                    g.tensor_tensor(T16[:, k, 1, :], a, mask[:, 0:1].to_broadcast([P, S]), ALU.add).then_inc(split_step, 1)
                    pool.wait_ge(split_step, b * 8 + 2 * k + 2)
                    g.tensor_tensor(T16[:, k, 2, :], a, T16[:, k, 1, :], ALU.subtract).then_inc(split_ok, 1)
            pool.wait_ge(xn_ok, B)
            pool.wait_ge(mod_ok, 1)
            for b in range(B):
                xb = X[:, b * TB:(b + 1) * TB, :]
                g.tensor_tensor(xb, xb, gtmp[:, 0, b:b + 1, :].to_broadcast([P, TB, D]), ALU.add).then_inc(res_ok, 1)

            pool.wait_ge(slots_ok, 1)
            pool.wait_ge(zero_out, 16 * 8)
            for t in range(NT):
                g.indirect_dma_start(x_sorted, bass.IndirectOffsetOnAxis(ap=slot[:, t:t + 1], axis=0), XH[:, t, :], None)\
                    .then_inc(sorted_out, 16)
            for k in range(2):
                pool.wait_ge(y_out[k], (SLOT_TILES // 2 + 1) * 16)
            for t in range(NT):
                g.indirect_dma_start(YG[:, t, :], None, y_sorted, bass.IndirectOffsetOnAxis(ap=slot[:, t:t + 1], axis=0))\
                    .then_inc(gathered[t // TB], 16)

        @block.scalar
        def _(act):
            a = nc.scalar
            row = lambda v: v.rearrange("(a n) -> a n", a=1)
            for r0, src in ((0, b1.rearrange("e (c f) -> (e c) f", f=P)), (32, gamma), (40, beta), (48, cent), (56, c),
                            (60, row(bq)), (61, row(bk))):
                act.dma_start(rows[r0:r0 + src.shape[0], :], src).then_inc(rows_in, 16)
            act.dma_start(bv_b[:, :], row(bv).to_broadcast([P, D])).then_inc(bias_in, 16)
            act.dma_start(bo_b[:, :], row(bo).to_broadcast([P, D])).then_inc(bias_in, 16)
            act.dma_start(lam_c[:, :], row(lam).to_broadcast([P, 1])).then_inc(bias_in, 16)
            act.dma_start(b2_b[:, :], row(b2.rearrange("e d -> (e d)")).to_broadcast([P, E * D])).then_inc(bias_in, 16)
            act.wait_ge(cols_ok, 1)
            a.activation(silu[:, 0, :], cols[:, 56:60], ACT.Exp, scale=-1.0).then_inc(silu_e, 1)
            act.wait_ge(stats_ok, 1)
            a.activation(lnt[:, 6, :], lnt[:, 5, :], ACT.Sqrt).then_inc(root_ok, 1)
            act.wait_ge(mod_ok, 1)
            act.sem_inc(exp_ok, SB_)
            act.sem_inc(ot_ok, 1)
            for half in range(2):
                act.sem_inc(ot_out[half], 16)
            bq_c, bk_c = cols[:, 60:61], cols[:, 61:62]
            with act.Fori(0, B) as b:
                act.wait_ge(xt_ps, b + 1)
                a.activation(HT[:, :], ps2(0), ACT.Identity, scale=modT[:, 1, bass.ds(b, 1)], bias=modT[:, 0, bass.ds(b, 1)])\
                    .then_inc(ht_ok, 1)
                act.wait_ge(q_ps, b + 1)
                a.activation(T32[:, 4, :], ps2(2), ACT.Tanh, bias=bq_c).then_inc(tanh_ok, 1)
                a.activation(T32[:, 0, :], ps2(2), ACT.Identity, scale=HD ** -0.5, bias=bqs[:, :])
                a.activation(T16[:, 0, 0, :], ps2(2), ACT.Identity, scale=HD ** -0.5, bias=bqs[:, :]).then_inc(first_ok, 1)
                act.wait_ge(k_ps, b + 1)
                a.activation(T32[:, 1, :], ps2(4), ACT.Identity, bias=bk_c)
                a.activation(T16[:, 1, 0, :], ps2(4), ACT.Identity, bias=bk_c).then_inc(first_ok, 1)
                a.activation(T32[:, 2, :], ps2(4), ACT.Tanh, bias=bk_c)
                a.activation(T16[:, 2, 0, :], ps2(4), ACT.Tanh, bias=bk_c).then_inc(first_ok, 1)
                act.wait_ge(qj_ps, b + 1)
                a.activation(T32[:, 3, :], ps2(0), ACT.Copy)
                a.activation(T16[:, 3, 0, :], ps2(0), ACT.Copy).then_inc(first_ok, 1)
                act.wait_ge(v_ps, b + 1)
                act.wait_ge(parts_out, (b + 1) * 12 * 16)

            def evacuate(b, g, half):
                act.wait_ge(pv_ok, (b * NG + g) * NU + max(u for u in HALF_END if HALF_END[u] == half) + 1 + EB)
                act.wait_ge(ot_out[half], (b * NG + g + 1) * 16)
                a.activation(OT[:, half, :], PS[:, 7, :], ACT.Copy).then_inc(ot_ok, 1)

            def attention(b):
                for g in range(NG):
                    for u, (qc, kb) in enumerate(UNITS):
                        off = max(0, kb - 4 * qc) * P
                        for h in range(HG):
                            n = u * HG + h
                            act.wait_ge(s_ps, (b * NG + g) * NU * HG + n + 1)
                            if h == 0:
                                act.wait_ge(pv_ok, (b * NG + g) * NU + u + 1)
                            a.activation(PT[:, u % EB, h, off:HALF], PS[:, 4 + n % SB_, off:HALF], ACT.Exp).then_inc(exp_ok, 1)
                        if u == LAG + 3:
                            evacuate(b, g, 0)
                        if u == LAG - 1 and g:
                            evacuate(b, g - 1, 1)
                evacuate(b, NG - 1, 1)
            act.wait_ge(zero_out, 16 * 8)
            with act.Fori(0, B) as b:
                attention(b)

            for k in range(16):
                act.wait_ge(w_tr, k + 1)
                dst = (W1T if k < 8 else W2T)[:, (k % 8) * HALF:(k % 8 + 1) * HALF]
                a.activation(dst, PS[:, 4 + k % 4, :], ACT.Copy).then_inc(w_ev, 1)
            for k in range(2):
                act.wait_ge(stats_ok, 2 + k)
                a.activation(lnt[:, 6, :], lnt[:, 5, :], ACT.Sqrt).then_inc(root_ok, 1)
                if k == 0:
                    for b in range(B):
                        act.wait_ge(h2t_ps, b + 1)
                        a.activation(AT[:, b * S:(b + 1) * S], ps2(2 * (b % 2)), ACT.Copy).then_inc(h2t_ok, 1)
            act.wait_ge(oh_ok, 1)
            a.activation(rs[:, 1, 0:NT], rs[:, 0, 0:NT], ACT.Exp, scale=-1.0).then_inc(alpha_e, 1)

            act.wait_ge(slots_ok, 1)
            act.sem_inc(xt_ok, 2)
            act.sem_inc(hr_ok, 2)
            for k in range(2):
                act.sem_inc(y_out[k], 16)

            def expert(n):
                return act.value_load(tile_e[0:1, bass.ds(n, 1)], min_val=0, max_val=E - 1)

            def scaled(n, j):
                e = expert(n)
                act.wait_ge(xsT_ps, n + 1 + 4)
                act.wait_ge(h_ps, n + 1)
                a.activation(XT[:, j % 2, :], PS[:, j % 2, 0:P], ACT.Identity, scale=cols[:, bass.ds(e + 32, 1)],
                             bias=cols[:, bass.ds(e + 40, 1)]).then_inc(xt_ok, 1)

            def hidden(n, j):
                e = expert(n)
                act.wait_ge(hT_ps, n + 1 + 2)
                act.wait_ge(y_ps, n + 1)
                for k in range(FC):
                    last = a.activation(HR[:, j % 2, k * P:(k + 1) * P], PS[:, 4 + j % 2, k * P:(k + 1) * P], ACT.Relu,
                                        bias=cols[:, bass.ds(e * FC + k, 1)])
                last.then_inc(hr_ok, 1)

            def store_y(n, j):
                act.wait_ge(ys_ok, n + 1 + 2)
                act.dma_start(y_sorted[bass.ds(n * P, P), :], YS[:, j % 2, :]).then_inc(y_out[j % 2], 16)

            def act_step(n, j, first=False, tx=True):
                if tx:
                    scaled(n + 2, j)
                hidden(n, j)
                if not first:
                    store_y(n - 2, j)
            scaled(0, 0)
            scaled(1, 1)
            act_step(0, 0, first=True)
            act_step(1, 1, first=True)
            with act.Fori(0, (SLOT_TILES - 4) // 4) as i:
                for j in range(4):
                    act_step(i * 4 + 2 + j, j)
            for n in (SLOT_TILES - 2, SLOT_TILES - 1):
                act_step(n, n, tx=False)
            store_y(SLOT_TILES - 2, 0)
            store_y(SLOT_TILES - 1, 1)

        @block.tensor
        def _(pe):
            t_ = nc.tensor
            mm = t_.matmul
            pe.sem_inc(pv_ok, EB)
            pe.wait_ge(consts_ok, 1)
            pe.wait_ge(rows_in, 7 * 16)
            t_.transpose(PS[:, 0, 0:62], rows[0:62, :], ident[0:62, 0:62]).then_inc(cols_ps, 1)
            pe.wait_ge(w_in, 5 * 16)
            for n in range(4):
                last = t_.transpose(PS[:, 1, n * P:(n + 1) * P], wraw[:, n, :], ident[:, :])
            last.then_inc(wT_ps, 1)
            pe.wait_ge(silu_ok, 1)
            for k in range(2):
                mm(PS[:, 2, k * B:(k + 1) * B], wm[:, k * D:(k + 1) * D], silu[:, 3, :], start=(k == 0), stop=True,
                   skip_group_check=True)
            for b in range(B):
                last = mm(PS[:, 4 + b, :], silu_b[:, b, :], wm[:, 2 * D:6 * D], start=True, stop=True)
            last.then_inc(mod_ps, 1)
            pe.wait_ge(wT_ok, 1)
            pe.wait_ge(mod_ok, 1)
            with pe.Fori(0, B) as b:
                pe.wait_ge(xn_ok, b + 1)
                for t in range(TB):
                    last = t_.transpose(ps2(0)[:, t * P:(t + 1) * P], XN[:, t, :], ident[:, :])
                last.then_inc(xt_ps, 1)
                pe.wait_ge(ht_ok, b + 1)
                for n, done in ((0, q_ps), (1, k_ps)):
                    for k in range(2):
                        last = mm(PS[:, 2 + 2 * n + k, :], wT[:, n, :], HT[:, k * HALF:(k + 1) * HALF], start=True, stop=True)
                    last.then_inc(done, 1)
                for t in range(TB):
                    last = mm(ps2(6)[:, t * P:(t + 1) * P], HT[:, t * P:(t + 1) * P], wT[:, 2, :], start=(t % 4 == 0), stop=True,
                              skip_group_check=True)
                last.then_inc(v_ps, 1)
                pe.wait_ge(tanh_ok, b + 1)
                for k in range(2):
                    last = mm(PS[:, k, :], JL[:, :], T32[:, 4, k * HALF:(k + 1) * HALF], start=True, stop=True)
                last.then_inc(qj_ps, 1)
                pe.wait_ge(first_ok, (b + 1) * 4)
                pe.wait_ge(va_ok, b + 1)

            def maximum(kind, g, k, index, slot_, loads, group):
                pe.wait_ge(max_used, index + 1)
                bank = 2 * slot_
                if kind == "T":
                    pe.wait_ge(m_parts_ok, group + 1)
                    t_.transpose(PS[:, bank, 0:P // 2].bitcast(BF16)[0:HG * 3 * TB, :],
                                 mparts[:, :, :, :].rearrange("p h j t -> p (h j t)"), identb[:, :]).then_inc(max_ps, 1)
                    return
                h, t = MTILES[k]
                if k == 0:
                    pe.wait_ge(stack_in[g], (loads + 1) * 10 * 16)
                n = (t + 1) * P
                for c0 in range(0, n, HALF):
                    c1 = min(n, c0 + HALF)
                    last = mm(PS[:, bank + c0 // HALF, 0:c1 - c0], SQ(g, h)[0:KROWS, t * P:(t + 1) * P],
                              SK(g, h)[0:KROWS, c0:c1], start=True, stop=True)
                last.then_inc(max_ps, 1)

            for i, (kind, ahead, k) in enumerate(FIRST):
                maximum(kind, ahead, k, i, i % MB_, 0, ahead)

            def products(b, g, u):
                qc, kb = UNITS[u]
                pe.wait_ge(exp_ok, ((b * NG + g) * NU + u + 1) * HG + SB_)
                if kb == 0:
                    pe.wait_ge(ot_ok, (b * NG + g) * 2 + qc + 1)
                off = max(0, kb - 4 * qc) * P
                for h in range(HG):
                    last = mm(PS[32 * h:32 * h + VW, 7, off:HALF],
                              Vs[:, g, (kb * HG + h) * VW:(kb * HG + h + 1) * VW], PT[:, u % EB, h, off:HALF],
                              start=(kb == 0), stop=(u in HALF_END), skip_group_check=True)
                last.then_inc(pv_ok, 1)

            def attention(b, b_last):
                trail = []
                for g in range(NG):
                    gi = b * NG + g
                    todo = list(items(g, b_last))
                    for u, (qc, kb) in enumerate(UNITS):
                        mine = [it for it in todo if it[1] == u]
                        if u == 0:
                            pe.wait_ge(m_in, (gi + 1) * HG * 16)
                        off = max(0, kb - 4 * qc) * P
                        for h in range(HG):
                            n = u * HG + h
                            pe.wait_ge(exp_ok, gi * NU * HG + n + 1)
                            bank = PS[:, 4 + n % SB_, :]
                            last = mm(bank[:, off:HALF], SK(g, h)[0:MROWS, kb * P:(kb + 1) * P],
                                      SQ(g, h)[0:MROWS, qc * HALF + off:(qc + 1) * HALF], start=True, stop=True, skip_group_check=True)
                            if u in DIAG:
                                last = mm(bank[:, off:off + P], identb[:, :], after[:, :], start=False, stop=True,
                                          skip_group_check=True)
                            last.then_inc(s_ps, 1)
                            for i, _, kind, place, ahead, k in mine[h * len(mine) // HG:(h + 1) * len(mine) // HG]:
                                skip = left_out(g, i) if b_last else 0
                                maximum(kind, place, k, use(b, g, i) - skip, (g * PER + i + len(FIRST) - skip) % MB_,
                                        b + (g + ahead) // NG, gi + ahead)
                        trail.append((g, u))
                        if len(trail) > LAG:
                            products(b, *trail.pop(0))
                for g, u in trail:
                    products(b, g, u)
            with pe.Fori(0, B - 1) as b:
                attention(b, False)
            attention(B - 1, True)

            for b in range(B):
                pe.wait_ge(at_ok, b + 1)
                for t in range(TB):
                    n = b * TB + t
                    last = mm(ps2(2 * b)[:, t * P:(t + 1) * P], AT[:, n * P:(n + 1) * P], WOG[:, b, :], start=(t % 4 == 0),
                              stop=True, skip_group_check=True)
                last.then_inc(o_ps, 1)
            pe.wait_ge(w12_in, 32)
            pe.wait_ge(x1_ok, B)
            for k in range(16):
                if k >= 4:
                    pe.wait_ge(w_ev, k - 3)
                for j in range(4):
                    n = (k % 8) * 4 + j
                    last = t_.transpose(PS[:, 4 + k % 4, j * P:(j + 1) * P], (W1r if k < 8 else W2r)[:, n, :], ident[:, :])
                last.then_inc(w_tr, 1)
            for b in range(B):
                pe.wait_ge(h2_ok, b + 1)
                if b >= 2:
                    pe.wait_ge(h2t_ok, b - 1)
                for t in range(TB):
                    last = t_.transpose(ps2(2 * (b % 2))[:, t * P:(t + 1) * P], H2[:, b * TB + t, :], ident[:, :])
                last.then_inc(h2t_ps, 1)
            pe.wait_ge(w_ev, 16)
            for b in range(B):
                pe.wait_ge(h2t_ok, b + 1)
                for t in range(TB):
                    n = b * TB + t
                    last = mm(PS[:, 4, n * E:(n + 1) * E], AT[:, n * P:(n + 1) * P], cols[:, 48:56], start=(n == 0), stop=True,
                              skip_group_check=True)
            last.then_inc(score_ps, 1)
            pe.wait_ge(oh_ok, 2)
            mm(PS[:, 5, 0:NT * E], triu[:, :], ohb[:, :], start=True, stop=True)
            mm(PS[:, 6, 0:NT * E], onesb[:, :], ohb[:, :], start=True, stop=True).then_inc(cnt_ps, 1)
            pe.wait_ge(slots_ok, 1)
            pe.sem_inc(xsT_ps, 4)
            pe.sem_inc(h_ps, 2)
            pe.sem_inc(hT_ps, 2)
            pe.sem_inc(y_ps, 2)

            def expert(n):
                return pe.value_load(tile_e[0:1, bass.ds(n, 1)], min_val=0, max_val=E - 1)

            def turn(n, j, q=None):
                pe.wait_ge(xs_in[j % 4], ((n // 4 if q is None else q) + 1) * 16)
                pe.wait_ge(xt_ok, n + 1)
                t_.transpose(PS[:, j % 2, 0:P], XS[:, j % 4, :], ident[:, :]).then_inc(xsT_ps, 1)

            def up(n, j):
                e = expert(n)
                pe.wait_ge(xt_ok, n + 1 + 2)
                pe.wait_ge(hs_ok, n + 1)
                mm(PS[:, 2 + j % 2, :], XT[:, j % 2, :], W1T[:, bass.ds(e * FF, FF)], start=True, stop=True).then_inc(h_ps, 1)

            def turn_hidden(n, j):
                pe.wait_ge(hs_ok, n + 1 + 2)
                pe.wait_ge(hr_ok, n + 1)
                for k in range(FC):
                    last = t_.transpose(PS[:, 4 + j % 2, k * P:(k + 1) * P], HS[:, j % 2, k * P:(k + 1) * P], ident[:, :])
                last.then_inc(hT_ps, 1)

            def down(n, j):
                e = expert(n)
                pe.wait_ge(hr_ok, n + 1 + 2)
                pe.wait_ge(ys_ok, n + 1)
                for k in range(FC):
                    last = mm(PS[:, 6 + j % 2, 0:D], HR[:, j % 2, k * P:(k + 1) * P],
                              W2T[:, bass.ds(e * FF + k * P, P)], start=(k == 0), stop=(k == FC - 1))
                last.then_inc(y_ps, 1)

            def pe_step(n, j, y=True, h=True, tx=True, q=None):
                if tx:
                    turn(n + 2, j + 2, q)
                if h:
                    up(n + 1, j + 1)
                turn_hidden(n, j)
                if y:
                    down(n - 1, j - 1)
            turn(0, 0)
            turn(1, 1)
            up(0, 0)
            pe_step(0, 0, y=False)
            pe_step(1, 1)
            with pe.Fori(0, (SLOT_TILES - 4) // 4) as i:
                for j in range(4):
                    pe_step(i * 4 + 2 + j, j + 2, q=i + 1)
            pe_step(SLOT_TILES - 2, SLOT_TILES - 2, tx=False)
            pe_step(SLOT_TILES - 1, SLOT_TILES - 1, tx=False, h=False)
            down(SLOT_TILES - 1, SLOT_TILES - 1)

        @block.vector
        def _(dve):
            v = nc.vector
            count = [0]

            def link(ins):
                count[0] += 1
                ins.then_inc(dve_chain, 1)
                dve.wait_ge(dve_chain, count[0])

            def tt(o, a, b_, op):
                return v.tensor_tensor(o, a, b_, op)

            def statistics(src, rounds):
                with dve.Fori(0, B) as b:
                    for t in range(TB):
                        last = v.bn_stats(stat[:, bass.ds(b * TB + t, 1), :].rearrange("p a k -> p (a k)"),
                                          src[:, bass.ds(b * TB + t, 1), :].rearrange("p a d -> p (a d)"))
                    last.then_inc(bn_ok, 1)
                dve.wait_ge(bn_ok, B * rounds)
                L = lambda k: lnt[:, k, :]
                tt(L(0), stat[:, :, 1], stat[:, :, 4], ALU.add)
                tt(L(2), stat[:, :, 2], stat[:, :, 5], ALU.add)
                link(tt(L(1), stat[:, :, 1], stat[:, :, 4], ALU.subtract))
                v.tensor_scalar(L(0), L(0), 0.5, None, ALU.mult)
                link(tt(L(3), L(1), L(1), ALU.mult))
                link(v.scalar_tensor_tensor(L(4), L(3), D / 4.0, L(2), ALU.mult, ALU.add))
                v.tensor_scalar(L(5), L(4), 1.0 / D, EPS, ALU.mult, ALU.add).then_inc(stats_ok, 1)
                dve.wait_ge(root_ok, rounds)
                link(v.reciprocal(L(7), L(6)))
                link(tt(L(8), L(5), L(7), ALU.mult))
                link(tt(L(8), L(8), L(6), ALU.add))
                link(v.tensor_scalar(L(8), L(8), 0.5, None, ALU.mult))
                link(v.reciprocal(L(9), L(8)))

            def normed(o, src, n):
                return v.tensor_scalar(o, src[:, bass.ds(n, 1), :].rearrange("p a d -> p (a d)"), lnt[:, 0, bass.ds(n, 1)],
                                       lnt[:, 9, bass.ds(n, 1)], ALU.subtract, ALU.mult)

            dve.sem_inc(max_used, MB_)
            dve.wait_ge(cols_ps, 1)
            v.tensor_copy(cols[:, 0:62], PS[:, 0, 0:62]).then_inc(cols_ok, 1)
            dve.wait_ge(cols_ok, 1)
            v.tensor_scalar(bqs[:, :], cols[:, 60:61], HD ** -0.5, None, ALU.mult)
            dve.wait_ge(silu_e, 1)
            link(v.tensor_scalar(silu[:, 1, :], silu[:, 0, :], 1.0, None, ALU.add))
            link(v.reciprocal(silu[:, 2, :], silu[:, 1, :]))
            link(tt(silu[:, 3, :], silu[:, 2, :], cols[:, 56:60], ALU.mult))
            v.tensor_copy(silu_b[:, :, :], silu[:, 3, :].unsqueeze(2).to_broadcast([P, B, P])).then_inc(silu_ok, 1)
            dve.wait_ge(wT_ps, 1)
            v.tensor_copy(wT[:, :, :].rearrange("p n d -> p (n d)"), PS[:, 1, :]).then_inc(wT_ok, 1)
            dve.wait_ge(x_in, 16)
            statistics(X, 1)
            dve.wait_ge(j_in, H * 16)
            dve.wait_ge(bias_in, 4 * 16)
            v.tensor_scalar(JL[:, :], JB[:, :], lam_c[:, :], None, ALU.mult)
            dve.wait_ge(mod_ps, 1)
            dve.wait_ge(wT_ok, 1)
            v.tensor_copy(modT[:, 0, :], PS[:, 2, 0:B])
            v.tensor_scalar(modT[:, 1, :], PS[:, 2, B:2 * B], 1.0, None, ALU.add)
            link(v.tensor_copy(MB[:, :, :, :].rearrange("p b k d -> p b (k d)"), PS[:, 4:8, :]))
            v.tensor_scalar(MB[:, :, 2, :], MB[:, :, 2, :], 1.0, None, ALU.add)
            for k in (0, 3):
                gate, sign, size = MB[:, :, k, :], gtmp[:, 0, :, :], gtmp[:, 1, :, :]
                link(v.tensor_scalar(sign, gate, 0.0, 2.0, ALU.is_ge, ALU.mult))
                v.scalar_tensor_tensor(size, gate, -1.0, gate, ALU.mult, ALU.max)
                link(v.tensor_scalar(sign, sign, 1.0, None, ALU.subtract))
                link(v.scalar_tensor_tensor(gate, size, 0.25, sign, ALU.max, ALU.mult))
            tt(WOG[:, :, :], MB[:, :, 0, :], wT[:, 3:4, :].to_broadcast([P, B, D]), ALU.mult)
            tt(gtmp[:, 0, :, :], MB[:, :, 0, :], bo_b[:, :].unsqueeze(1).to_broadcast([P, B, D]), ALU.mult).then_inc(mod_ok, 1)
            dve.wait_ge(mod_ok, 1)

            with dve.Fori(0, B) as b:
                for t in range(TB):
                    last = normed(XN[:, t, :], X, b * TB + t)
                last.then_inc(xn_ok, 1)
                dve.wait_ge(v_ps, b + 1)
                tt(VA[:, :, :, 0:HD], ps2(6).rearrange("p (t h w) -> p t h w", t=TB, h=H),
                   bv_b[:, :].rearrange("p (h w) -> p h w", h=H).unsqueeze(1).to_broadcast([P, TB, H, HD]), ALU.add).then_inc(va_ok, 1)
                dve.wait_ge(xt_ps, b + 1)
                dve.wait_ge(v_out, (b + 1) * NG * 16)

            def maximum(kind, place, k, index, slot_, group):
                dve.wait_ge(max_ps, index + 1)
                bank = 2 * slot_
                if kind == "T":
                    if not (isinstance(group, int) and group == 0):
                        dve.wait_ge(m_in, group * HG * 16)
                    v.tensor_copy(mrow[:, :], PS[:, bank, 0:P // 2].bitcast(BF16)[0:HG * 3 * TB, :]).then_inc(max_used, 1)
                    return
                h, t = MTILES[k]
                n = (t + 1) * P
                src = ps2(bank)[:, 0:n]
                dve.sem_inc(max_seen, 1)
                v.tensor_tensor_reduce(out=src, in0=src, in1=mask[:, S - n:S], scale=1.0, scalar=-3e38, op0=ALU.add, op1=ALU.max,
                                       accum_out=maxima[:, place, h * TB + t:h * TB + t + 1]).then_inc(max_used, 1)
                if k == NM - 1:
                    m = maxima[:, place, :].rearrange("p (h t) -> p h t", h=HG)
                    rest = mres[:, 0, :].rearrange("p (h t) -> p h t", h=HG)
                    dve.wait_ge(max_used, index + 1 + MB_)
                    for step, ins in enumerate((
                            lambda: v.tensor_scalar(mparts[:, :, 0, :], m, -1.0, None, ALU.mult),
                            lambda: v.scalar_tensor_tensor(rest, m, -1.0, mparts[:, :, 0, :], ALU.mult, ALU.subtract),
                            lambda: v.tensor_copy(mparts[:, :, 1, :], rest))):
                        ins().then_inc(m_split, 1)
                        dve.wait_ge(m_split, group * 3 + step + 1)
                    tt(mparts[:, :, 2, :], rest, mparts[:, :, 1, :], ALU.subtract).then_inc(m_parts_ok, 1)

            for i, (kind, ahead, k) in enumerate(FIRST):
                maximum(kind, ahead, k, i, i % MB_, ahead)

            def attention(b, b_last):
                for g in range(NG):
                    for i, _, kind, place, ahead, k in items(g, b_last):
                        skip = left_out(g, i) if b_last else 0
                        maximum(kind, place, k, use(b, g, i) - skip, (g * PER + i + len(FIRST) - skip) % MB_, b * NG + g + ahead)
            with dve.Fori(0, B - 1) as b:
                attention(b, False)
            attention(B - 1, True)

            dve.wait_ge(num_in, 2 * B * 16)
            for b in range(B):
                part = slice(b * S, (b + 1) * S)
                link(v.reciprocal(DEN[:, part], DEN[:, part]))
                tt(AT[:, part], NUM[:, part], DEN[:, part], ALU.mult).then_inc(at_ok, 1)
            dve.wait_ge(res_ok, B)
            flat = lambda r: r.rearrange("p t d -> p (t d)")
            tiles = lambda b: slice(b * TB, (b + 1) * TB)
            for b in range(B):
                dve.wait_ge(o_ps, b + 1)
                xb = flat(X[:, tiles(b), :])
                tt(xb, xb, ps2(2 * b), ALU.add).then_inc(x1_ok, 1)
            dve.wait_ge(x1_ok, B)
            dve.wait_ge(at_ok, B)
            statistics(X, 2)
            over = lambda b, k: MB[:, b, k:k + 1, :].to_broadcast([P, TB, D])
            for b in range(B):
                for t in range(TB):
                    n = b * TB + t
                    last = normed(H2[:, n, :], X, n)
                link(last)
                hb = H2[:, tiles(b), :]
                link(tt(hb, hb, over(b, 2), ALU.mult))
                tt(hb, hb, over(b, 1), ALU.add).then_inc(h2_ok, 1)
            dve.wait_ge(h2_ok, B)
            statistics(H2, 3)
            for n in range(NT):
                last = normed(XH[:, n, :], H2, n)
            link(last)

            dve.wait_ge(score_ps, 1)
            link(v.tensor_copy(sc[:, :, :].rearrange("p t e -> p (t e)"), PS[:, 4, 0:NT * E]))
            best, idx = rs[:, 0, 0:NT], rs[:, 2, 0:NT]
            col = lambda r: r.unsqueeze(2).to_broadcast([P, NT, E])
            link(v.tensor_reduce(best, sc[:, :, :], AX.X, ALU.max))
            link(tt(rt[:, 0, :, :], sc[:, :, :], col(best), ALU.is_ge))
            link(v.scalar_tensor_tensor(rt[:, 1, :, :], rt[:, 0, :, :], -float(E), iota_e[:, :].unsqueeze(1).to_broadcast([P, NT, E]),
                                        ALU.mult, ALU.add))
            link(v.tensor_reduce(idx, rt[:, 1, :, :], AX.X, ALU.min))
            onehot = rt[:, 2, :, :]
            link(tt(onehot, rt[:, 1, :, :], col(idx), ALU.is_equal))
            dve.sem_inc(oh_ok, 1)
            v.tensor_copy(ohb[:, :], onehot.rearrange("p t e -> p (t e)")).then_inc(oh_ok, 1)
            dve.wait_ge(alpha_e, 1)
            link(v.tensor_scalar(rs[:, 3, 0:NT], rs[:, 1, 0:NT], 1.0, None, ALU.add))
            link(v.reciprocal(rs[:, 4, 0:NT], rs[:, 3, 0:NT]))
            alpha = rs[:, 4, :]
            dve.wait_ge(cnt_ps, 1)
            within = PS[:, 5, 0:NT * E].rearrange("p (t e) -> p t e", e=E)
            link(v.tensor_copy(rt[:, 3, :, :].rearrange("p t e -> p (t e)"), PS[:, 6, 0:NT * E]))
            v.memset(rs[:, 5, :], 1.0)
            link(v.memset(rt[:, 6, :, :], 0.0))
            for e in range(E):
                last = v.tensor_tensor_scan(rt[:, 4, :, e], rs[:, 5, 0:NT], rt[:, 3, :, e], 0.0, ALU.mult, ALU.add)
            link(last)
            few = rt[:, 6, :, :].rearrange("p t e -> p (t e)")
            link(tt(rt[:, 5, :, :].rearrange("p t e -> p (t e)").rearrange("p (e t) -> p e t", e=E),
                    rt[:, 4, NT - 1, :].unsqueeze(2).to_broadcast([P, E, NT]),
                    iota_n[:, :].unsqueeze(1).to_broadcast([P, E, NT]), ALU.is_gt))
            link(v.tensor_reduce(few[:, 0:E], rt[:, 5, :, :].rearrange("p t e -> p (t e)").rearrange("p (e t) -> p e t", e=E), AX.X, ALU.add))
            link(v.tensor_tensor_scan(few[:, E:2 * E], rs[:, 5, 0:E], few[:, 0:E], 0.0, ALU.mult, ALU.add))
            link(tt(few[:, 2 * E:3 * E], few[:, E:2 * E], few[:, 0:E], ALU.subtract))
            link(tt(rt[:, 4, :, :], rt[:, 4, :, :], rt[:, 3, :, :], ALU.subtract))
            link(tt(rt[:, 4, :, :], rt[:, 4, :, :], within, ALU.add))
            link(v.scalar_tensor_tensor(rt[:, 4, :, :], few[:, 2 * E:3 * E].unsqueeze(1).to_broadcast([P, NT, E]), float(P),
                                        rt[:, 4, :, :], ALU.mult, ALU.add))
            link(tt(rt[:, 4, :, :], rt[:, 4, :, :], onehot, ALU.mult))
            link(v.tensor_reduce(rs[:, 6, 0:NT], rt[:, 4, :, :], AX.X, ALU.add))
            v.tensor_copy(slot[:, :], rs[:, 6, 0:NT])
            cmp_ = rt[:, 7, :, :].rearrange("p t e -> p (t e)")
            ne = E - 1
            for t0 in range(0, SLOT_TILES, 20):
                link(tt(cmp_[:, 0:20 * ne].rearrange("p (t e) -> p t e", e=ne),
                        few[:, E:2 * E - 1].unsqueeze(1).to_broadcast([P, 20, ne]),
                        iota_t[:, t0:t0 + 20].unsqueeze(2).to_broadcast([P, 20, ne]), ALU.is_le))
                link(v.tensor_reduce(rs[:, 7, t0:t0 + 20], cmp_[:, 0:20 * ne].rearrange("p (t e) -> p t e", e=ne), AX.X, ALU.add))
            v.tensor_copy(tile_e[:, :], rs[:, 7, :]).then_inc(slots_ok, 1)

            dve.wait_ge(slots_ok, 1)
            dve.sem_inc(hs_ok, 2)
            dve.sem_inc(ys_ok, 2)

            def raw(n, j):
                dve.wait_ge(h_ps, n + 1 + 2)
                dve.wait_ge(hT_ps, n + 1)
                v.tensor_copy(HS[:, j % 2, :], PS[:, 2 + j % 2, :]).then_inc(hs_ok, 1)

            def biased(n, j, q=None):
                e = dve.value_load(tile_e[0:1, bass.ds(n, 1)], min_val=0, max_val=E - 1)
                dve.wait_ge(y_ps, n + 1 + 2)
                dve.wait_ge(y_out[j % 2], ((n // 2 if q is None else q) + 1) * 16)
                tt(YS[:, j % 2, :], PS[:, 6 + j % 2, 0:D], b2_b[:, bass.ds(e * D, D)], ALU.add).then_inc(ys_ok, 1)
            raw(0, 0)
            raw(1, 1)
            with dve.Fori(0, (SLOT_TILES - 4) // 4) as i:
                for j in range(4):
                    raw(i * 4 + 2 + j, j)
                    biased(i * 4 + j, j, i * 2 + j // 2)
            for n in range(SLOT_TILES - 4, SLOT_TILES):
                if n + 2 < SLOT_TILES:
                    raw(n + 2, n)
                biased(n, n)

            for b in range(B):
                dve.wait_ge(gathered[b], TB * 16)
                for t in range(TB):
                    n = b * TB + t
                    last = v.scalar_tensor_tensor(YG[:, n, :], YG[:, n, :], alpha[:, n:n + 1], H2[:, n, :], ALU.mult, ALU.add)
                link(last)
                yb = YG[:, tiles(b), :]
                link(tt(yb, yb, over(b, 3), ALU.mult))
                tt(yb, yb, X[:, tiles(b), :], ALU.add).then_inc(fin_ok, 1)


_INS = ['L0_attn_x', 'L0_attn_Wq', 'L0_attn_bq', 'L0_attn_Wk', 'L0_attn_bk', 'L0_attn_Wv', 'L0_attn_bv', 'L0_attn_Wo',
        'L0_attn_bo', 'L0_attn_J_attn', 'L0_attn_lambda_attn', 'L0_ffn_centroids', 'L0_ffn_gamma', 'L0_ffn_beta',
        'L0_ffn_W1', 'L0_ffn_b1', 'L0_ffn_W2', 'L0_ffn_b2', 'L0_c', 'L0_wmod']
_OUTS = [((B, S, D), 'float32')]


def kernel(**inputs):
    import numpy as _np
    import concourse.bacc as _bacc
    from concourse import mybir as _mybir
    from concourse.bass_utils import run_bass_kernel_spmd as _run

    nc = _bacc.Bacc("TRN2", target_bir_lowering=False, num_devices=1)
    arrays, args = {}, []
    for name in _INS:
        a = _np.ascontiguousarray(inputs[name])
        if a.ndim == 0:
            a = a.reshape(1)
        arrays[f"in_{name}_dram"] = a
        args.append(nc.dram_tensor(f"in_{name}_dram", a.shape, _mybir.dt.from_np(a.dtype), kind="ExternalInput").ap())
    for i, (shape, dtype) in enumerate(_OUTS):
        dt = _mybir.dt.from_np(_np.dtype(dtype))
        args.append(nc.dram_tensor(f"out_{i}_dram", shape, dt, kind="ExternalOutput").ap())
    build(nc, *args)
    r = _run(nc, [arrays], core_ids=[0])
    got = tuple(r.results[0][f"out_{i}_dram"] for i in range(len(_OUTS)))
    return got[0]
```

```python
import concourse.bass as bass
from concourse import mybir
from contextlib import ExitStack

F32 = mybir.dt.float32
BF16 = mybir.dt.bfloat16
I32 = mybir.dt.int32
ALU = mybir.AluOpType
ACT = mybir.ActivationFunctionType
AX = mybir.AxisListType

B, S, D = 4, 1024, 128
H, HD = 16, 8
E, FF = 8, 512
P = 128
TB = S // P
NT = B * TB
HG = 4
NG = H // HG
GROUPS = B * NG
HALF = 512
EPS = 1e-5
BIG = 1e30
FC = FF // P
SLOT_TILES = (B * S + E * (P - 1)) // P + 1
assert SLOT_TILES == 40
ROW = 2 * HD
TERMS = 6
KROWS = ROW * TERMS
MROWS = KROWS + 3
VW = HD + 1


def build(nc, x, Wq, bq, Wk, bk, Wv, bv, Wo, bo, J, lam, cent, gamma, beta, W1, b1, W2, b2, c, wmod, out):
    ctx = ExitStack()
    with ctx:
        def sb(name, shape, dt=F32):
            return ctx.enter_context(nc.sbuf_tensor(name, shape, dt))

        def sem(name):
            return ctx.enter_context(nc.semaphore(name))

        def dram(name, shape, dt=F32):
            return nc.dram_tensor(name, shape, dt, kind="Internal").ap()

        q_parts = dram("q_parts", [B, H, 3, ROW, S], BF16)
        k_parts = dram("k_parts", [B, H, 3, ROW, S], BF16)
        o_raw = dram("o_raw", [B, NG, P, S])
        x_sorted = dram("x_sorted", [SLOT_TILES * P, D])
        y_sorted = dram("y_sorted", [SLOT_TILES * P, D])

        X = sb("X", [P, NT, D])
        ident = sb("ident", [P, P])
        identb = sb("identb", [P, P], BF16)
        mask = sb("mask", [P, S])
        wT = sb("wT", [P, 4, D])
        rows = sb("rows", [64, D])
        cols = sb("cols", [P, 64])
        JB = sb("JB", [P, P])
        JL = sb("JL", [P, P])
        lam_c = sb("lam_c", [P, 1])
        bqs = sb("bqs", [P, 1])
        bv_b = sb("bv_b", [P, D])
        bo_b = sb("bo_b", [P, D])
        silu = sb("silu", [P, 4, B])
        modT = sb("modT", [P, 2, B])
        MB = sb("MB", [P, B, 4, D])
        gtmp = sb("gtmp", [P, 2, B, D])
        stat = sb("stat", [P, NT, 6])
        lnt = sb("lnt", [P, 12, NT])
        maxima = sb("maxima", [P, 4, HG * TB])
        mres = sb("mres", [P, 2, HG * TB])
        mparts = sb("mparts", [P, HG, 3, TB], BF16)
        mrow = sb("mrow", [HG * 3 * TB, P], BF16)
        HT = sb("HT", [P, S])
        OT = sb("OT", [P, 2, HALF])
        Vs = sb("Vs", [P, 4, TB * HG * VW])
        b2_b = sb("b2_b", [P, E * D])
        arenaA = sb("arenaA", [P, 24576])
        arenaB = sb("arenaB", [P, 12544])
        Aap = arenaA[:, :]
        Bap = arenaB[:, :]
        stacks = Aap[:, 0:16384].bitcast(BF16).rearrange("p (r s h q) -> p r s h q", r=4, s=2, h=HG)
        SQ = lambda r, h: stacks[:, r, 0, h, :]
        SK = lambda r, h: stacks[:, r, 1, h, :]
        PT = Aap[:, 16384:24576].rearrange("p (r h q) -> p r h q", r=4, h=HG)
        wraw = Aap[:, 16384:16896].rearrange("p (n d) -> p n d", n=4)
        silu_b = Aap[:, 16896:17408].rearrange("p (b d) -> p b d", b=B)
        wm = Aap[:, 17408:18176]
        NUM = Aap[:, 0:4096]
        DEN = Aap[:, 4096:8192]
        H2 = Aap[:, 0:4096].rearrange("p (t d) -> p t d", d=D)
        XH = Aap[:, 4096:8192].rearrange("p (t d) -> p t d", d=D)
        YG = Aap[:, 8192:12288].rearrange("p (t d) -> p t d", d=D)
        AT = Aap[:, 12288:16384]
        W1r = Aap[:, 16384:20480].rearrange("p (k d) -> p k d", d=D)
        W2r = Aap[:, 20480:24576].rearrange("p (k d) -> p k d", d=D)
        T32 = Bap[:, 0:5120].rearrange("p (k s) -> p k s", k=5)
        T16 = Bap[:, 5120:11264].bitcast(BF16).rearrange("p (k j s) -> p k j s", k=4, j=3)
        VA = Bap[:, 11264:11264 + TB * H * VW].rearrange("p (g t h w) -> p g t h w", g=NG, t=TB, h=HG)
        XN = T32[:, 3, :].rearrange("p (t d) -> p t d", d=D)
        W1T = Bap[:, 0:4096]
        W2T = Bap[:, 4096:8192]
        FB = 8192
        XS = Bap[:, FB:FB + 512].rearrange("p (r d) -> p r d", r=4)
        XT = Bap[:, FB + 512:FB + 768].rearrange("p (r d) -> p r d", r=2)
        W1C = Bap[:, FB + 768:FB + 1792].rearrange("p (r d) -> p r d", r=2)
        HR = Bap[:, FB + 1792:FB + 2816].rearrange("p (r d) -> p r d", r=2)
        YS = Bap[:, FB + 2816:FB + 3072].rearrange("p (r d) -> p r d", r=2)
        WOG = sb("WOG", [P, B, D])
        triu = sb("triu", [P, P], BF16)
        onesb = sb("onesb", [P, P], BF16)
        after = sb("after", [P, P], BF16)
        iota_e = sb("iota_e", [P, E])
        iota_t = sb("iota_t", [P, SLOT_TILES])
        iota_n = sb("iota_n", [P, NT])
        iotai = sb("iotai", [P, 96], I32)
        sc = Aap[:, 18432:18688].rearrange("p (t e) -> p t e", e=E)
        rt = Aap[:, 16384:18432].rearrange("p (k t e) -> p k t e", k=8, e=E)
        rs = Aap[:, 18688:19008].rearrange("p (k t) -> p k t", k=8)
        ohb = sb("ohb", [P, NT * E], BF16)
        slot = sb("slot", [P, NT], I32)
        tile_e = sb("tile_e", [P, SLOT_TILES], I32)
        zero = Aap[:, 18176:18176 + SLOT_TILES * D // 8]
        PS = ctx.enter_context(nc.psum_tensor("PS", [P, 8, HALF], F32))

        ps2 = lambda k: PS[:, k:k + 2, :].rearrange("p a b -> p (a b)")

        (w_in, rows_in, bias_in, j_in, consts_ok, pool_chain, dve_chain, cols_ps, cols_ok, silu_e, silu_ok,
         mod_ps, mod_ok, wT_ps, wT_ok, stats_ok, root_ok, xn_ok, ht_ok, q32_ok, tanh_ok, k32_ok,
         j32_ok, first_ok, split_step, split_ok, va_ok, parts_out, max_ps, max_used, m_split,
         m_parts_ok, m_in, s_ps, exp_ok, pv_ok, ot_ok, num_in, at_ok, o_ps, x1_ok, w12_in, w_tr, w_ev,
         h2_ok, h2t_ps, h2t_ok, score_ps, alpha_e, oh_ok, cnt_ps, slots_ok, zero_out, sorted_out, xsT_ps,
         xt_ok, h_ps, w1_ok, hr_ok, y_ps, ys_ok, fin_ok, out_done, res_ok, bn_ok, max_seen, stores_step, stored, split0_ok, split0_step, parts0_out, modT_ok, split0_q) = [sem(n) for n in (
            "w_in rows_in bias_in j_in consts_ok pool_chain dve_chain cols_ps cols_ok silu_e silu_ok mod_ps "
            "mod_ok wT_ps wT_ok stats_ok root_ok xn_ok ht_ok q32_ok tanh_ok k32_ok j32_ok first_ok "
            "split_step split_ok va_ok parts_out max_ps max_used m_split m_parts_ok m_in s_ps exp_ok "
            "pv_ok ot_ok num_in at_ok o_ps x1_ok w12_in w_tr w_ev h2_ok h2t_ps h2t_ok score_ps alpha_e oh_ok "
            "cnt_ps slots_ok zero_out sorted_out xsT_ps xt_ok h_ps w1_ok hr_ok y_ps ys_ok fin_ok out_done "
            "res_ok bn_ok max_seen stores_step stored split0_ok split0_step parts0_out modT_ok split0_q").split()]

        stack_in = [sem(f"stack_in{g}") for g in range(NG)]
        x_in = [sem(f"x_in{b}") for b in range(B)]
        ot_out = [sem(f"ot_out{k}") for k in range(2)]
        xs_in = [sem(f"xs_in{k}") for k in range(4)]
        y_out = [sem(f"y_out{k}") for k in range(2)]
        gathered = [sem(f"gathered{b}") for b in range(B)]

        block = ctx.enter_context(nc.Block())

        UNITS = [(qc, kb) for qc in range(2) for kb in range(4 * qc + 4)]
        NU = len(UNITS)
        DIAG = [u for u, (qc, kb) in enumerate(UNITS) if kb >= 4 * qc]
        HALF_END = {max(u for u, (qc, _) in enumerate(UNITS) if qc == q): q for q in range(2)}
        LAG = 2
        SB_, EB, MB_ = 3, 4, 2
        MTILES = [(h, t) for h in range(HG) for t in range(TB)]
        NM = len(MTILES)
        EARLY = 8
        SEQ = [("m", 1, k) for k in range(EARLY, NM)] + [("m", 2, 0), ("m", 2, 1), ("T", 1, 0)] + \
              [("m", 2, k) for k in range(2, EARLY)]
        PREP = ("X", "Q", "K", "V0", "V1", "J")
        PREP_AT = (10, 12, 14, 16, 18, 20)
        FIRST = [("P", 0, k) for k in range(len(PREP))] + [("m", 0, k) for k in range(NM)] + \
                [("m", 1, 0), ("m", 1, 1), ("T", 0, 0)] + [("m", 1, k) for k in range(2, EARLY)]

        SLOT_COST = [64 + HALF - max(0, kb - 4 * qc) * P for qc, kb in UNITS for h in range(HG)]

        def schedule(last):
            groups, n = [], 0
            for g in range(NG):
                seq = list(SEQ)
                if g == 0 and not last:
                    for k, at in reversed(list(enumerate(PREP_AT))):
                        seq.insert(at, ("P", 0, k))
                seq = [it for it in seq if not last or g + it[1] < NG]
                cost = [96 + dict(m=(MTILES[k % NM][1] + 1) * P, T=0, P=S)[kind] for kind, _, k in seq]
                at = [sum(SLOT_COST[:i + 1]) / sum(SLOT_COST) for i in range(NU * HG)]
                slots = [next(i for i in range(NU * HG) if sum(cost[:n]) / sum(cost) < at[i]) for n in range(len(seq))]
                groups.append([(n + i, slots[i], kind, (g + ahead) % NG, ahead, k) for i, (kind, ahead, k) in enumerate(seq)])
                n += len(seq)
            return groups, n
        ITEMS, PER = schedule(False)
        LAST_ITEMS, _ = schedule(True)
        N0 = len(FIRST)
        T_USE = lambda g, last: next(it[0] for it in (LAST_ITEMS if last else ITEMS)[g] if it[2] == "T")
        P_UNIT = {PREP[it[5]]: it[1] // HG + 1 for it in ITEMS[0] if it[2] == "P"}
        T_FIRST = FIRST.index(("T", 0, 0))

        assert PER % MB_ == 0 and (NU * HG) % SB_ == 0 and NU % EB == 0
        TENSORS = ((0, q_parts, 0), (2, k_parts, HD), (1, k_parts, 0), (3, q_parts, HD))
        PARTS_OUT = 12 * 16

        @block.sync
        def _(sp):
            sp.dma_start(wm[:, :], wmod).then_inc(w_in, 16)
            for n, w in enumerate((Wq, Wk, Wv, Wo)):
                sp.dma_start(wraw[:, n, :], w).then_inc(w_in, 16)
            for b in range(B):
                sp.dma_start(X[:, b * TB:(b + 1) * TB, :], x[b].rearrange("(t p) d -> p t d", p=P)).then_inc(x_in[b], 16)
            sp.wait_ge(pool_chain, 1)
            for h in range(H):
                sp.dma_start(JB[h * HD:(h + 1) * HD, h * HD:(h + 1) * HD], J[h]).then_inc(j_in, 16)
            Q_ROWS = ((0, 0, 3), (3, 0, 2), (5, 0, 1))
            K_ROWS = ((0, 0, 1), (1, 0, 1), (2, 0, 1), (3, 1, 1), (4, 1, 1), (5, 2, 1))

            def load_group(b, g):
                for side, src, terms in ((0, q_parts, Q_ROWS), (1, k_parts, K_ROWS)):
                    for t, j, n in terms:
                        sp.dma_start(stacks[t * ROW:(t + n) * ROW, g, side, :, :],
                                     src[bass.ds(b, 1), g * HG:(g + 1) * HG, j:j + n, :, :].rearrange("a h j r q -> (a j r) h q"))\
                            .then_inc(stack_in[g], 16)
                sp.dma_start(Vs[:, g, :], VA[:, g, :, :, :].rearrange("p t h w -> p (t h w)"))\
                    .then_inc(stack_in[g], 16)

            def send_maxima(g, index):
                sp.wait_ge(max_used, index + 1 + MB_)
                for h in range(HG):
                    sp.dma_start(stacks[KROWS:MROWS, g, 0, h, :].rearrange("r (t q) -> r t q", t=TB),
                                 mrow[h * 3 * TB:(h + 1) * 3 * TB, :]).then_inc(m_in, 16)

            def store_half(b, g, half):
                sp.wait_ge(ot_ok, (b * NG + g) * 2 + half + 2)
                sp.dma_start(o_raw[bass.ds(b, 1), g, :, half * HALF:(half + 1) * HALF].rearrange("a p q -> (a p) q"),
                             OT[:, half, :]).then_inc(ot_out[half], 16)

            def prepared(b):
                sp.wait_ge(stored, b + 1)
                sp.wait_ge(va_ok, b + 1)

            for n, (k, dst, off) in enumerate(TENSORS):
                if n:
                    sp.wait_ge(split0_ok, n)
                else:
                    sp.wait_ge(split0_q, 1)
                for j in range(3):
                    sp.dma_start(dst[0, :, j, off:off + HD, :], T16[:, k, j, :]).then_inc(parts0_out, 16)
            prepared(0)
            for g in range(NG):
                load_group(0, g)
            send_maxima(0, T_FIRST)

            def attention(b, last):
                for g in range(NG):
                    store_half(b, g, 0)
                    if not last or g + 1 < NG:
                        send_maxima((g + 1) % NG, b * PER + N0 + T_USE(g, last))
                    store_half(b, g, 1)
                    if not last and g:
                        if g == 1:
                            prepared(b + 1)
                        for place in (0, 1) if g == 1 else (g,):
                            sp.wait_ge(pv_ok, (b * NG + place + 1) * NU + EB)
                            load_group(b + 1, place)
            with sp.Fori(0, B - 1) as b:
                attention(b, False)
            attention(B - 1, True)

            for half in range(2):
                sp.wait_ge(ot_out[half], (GROUPS + 1) * 16)
            sp.wait_ge(pv_ok, GROUPS * NU + EB)
            for b in range(B):
                o_b = o_raw[b].rearrange("g (h r) q -> (g h) r q", h=HG)
                sp.dma_start(NUM[:, b * S:(b + 1) * S], o_b[:, 0:HD, :]).then_inc(num_in, 16)
                sp.dma_start(DEN[:, b * S:(b + 1) * S], o_b[:, HD:VW, :].to_broadcast([H, HD, S])).then_inc(num_in, 16)
            sp.dma_start(W1r, W1.rearrange("e (c f) d -> f (e c) d", f=P)).then_inc(w12_in, 16)
            sp.dma_start(W2r.rearrange("p (e c) f -> p e (c f)", e=E), W2.rearrange("e d n -> d e n")).then_inc(w12_in, 16)

            sp.wait_ge(sorted_out, NT * 16)
            with sp.Fori(0, SLOT_TILES // 4) as i:
                for j in range(4):
                    sp.wait_ge(xsT_ps, i * 4 + j + 1)
                    sp.dma_start(XS[:, j, :], x_sorted[bass.ds((i * 4 + j) * P, P), :]).then_inc(xs_in[j], 16)
            for b in range(B):
                sp.wait_ge(fin_ok, b + 1)
                sp.dma_start(out[b].rearrange("(t p) d -> p t d", p=P), YG[:, b * TB:(b + 1) * TB, :]).then_inc(out_done, 16)
            sp.wait_ge(out_done, B * 16)

        @block.gpsimd
        def _(pool):
            g = nc.gpsimd
            g.memset(ident[:, :], 0.0)
            g.memset(mask[:, :], 0.0)
            g.memset(triu[:, :], 1.0)
            g.memset(onesb[:, :], 1.0)
            g.memset(after[:, :], 0.0)
            g.memset(JB[:, :], 0.0)
            g.iota(iotai[:, 0:SLOT_TILES], [[1, SLOT_TILES]], base=0, channel_multiplier=0)
            g.iota(iotai[:, 48:48 + NT], [[P, NT]], base=0, channel_multiplier=0).then_inc(pool_chain, 1)
            pool.wait_ge(pool_chain, 1)
            g.affine_select(out=ident[:, :], in_=ident[:, :], compare_op=ALU.not_equal, fill=1.0, base=0,
                            pattern=[[-1, P]], channel_multiplier=1)
            g.affine_select(out=mask[:, S - P:S], in_=mask[:, S - P:S], compare_op=ALU.is_ge, fill=-BIG, base=0,
                            pattern=[[-1, P]], channel_multiplier=1)
            g.affine_select(out=after[:, :], in_=after[:, :], compare_op=ALU.is_ge, fill=-BIG, base=0,
                            pattern=[[1, P]], channel_multiplier=-1)
            g.affine_select(out=triu[:, :], in_=triu[:, :], compare_op=ALU.is_gt, fill=0.0, base=0,
                            pattern=[[1, P]], channel_multiplier=-1).then_inc(pool_chain, 1)
            pool.wait_ge(pool_chain, 2)
            g.tensor_copy(iota_e[:, :], iotai[:, 0:E])
            g.tensor_copy(iota_t[:, :], iotai[:, 0:SLOT_TILES])
            g.tensor_copy(iota_n[:, :], iotai[:, 48:48 + NT])
            g.memset(zero[:, :], 0.0)
            g.memset(VA.rearrange("p g t h w -> p (g t h) w")[:, :, HD:VW], 1.0).then_inc(pool_chain, 1)
            for r in range(NG):
                pool.wait_ge(pool_chain, 3 + r)
                g.memset(stacks[KROWS:MROWS, r, 1, :, :], 1.0).then_inc(pool_chain, 1)
            pool.wait_ge(pool_chain, 3 + NG)
            g.tensor_copy(identb[:, :], ident[:, :]).then_inc(consts_ok, 1)
            pool.wait_ge(consts_ok, 1)
            for k in range(8):
                pool.dma_start(x_sorted.rearrange("(k p t) d -> k p (t d)", k=8, p=P)[k], zero[:, :]).then_inc(zero_out, 16)

            def split(b, n, done_sem):
                k = TENSORS[n][0]
                pool.wait_ge(first_ok, b * 4 + n + 1)
                a = T32[:, k, :]
                g.tensor_tensor(a, a, T16[:, k, 0, :], ALU.subtract).then_inc(split_step, 1)
                done = b * 8 - 6 + 2 * n if not isinstance(b, int) else 2 * n
                pool.wait_ge(split_step, done + 1)
                g.tensor_tensor(T16[:, k, 1, :], a, mask[:, 0:1].to_broadcast([P, S]), ALU.add).then_inc(split_step, 1)
                pool.wait_ge(split_step, done + 2)
                g.tensor_tensor(T16[:, k, 2, :], a, T16[:, k, 1, :], ALU.subtract).then_inc(done_sem, 1)
            split(0, 0, split0_q)
            pool.wait_ge(parts0_out, PARTS_OUT)
            pool.sem_inc(stored, 1)
            with pool.Fori(1, B) as b:
                for n, (k, dst, off) in enumerate(TENSORS):
                    split(b, n, split_ok)
                    pool.wait_ge(split_ok, b * 4 + n - 3)
                    pool.sem_inc(stores_step, 1)
                    for j in range(3):
                        pool.dma_start(dst[bass.ds(b, 1), :, j, off:off + HD, :].rearrange("a h r q -> (a h) r q"),
                                       T16[:, k, j, :]).then_inc(parts_out, 16)
                pool.wait_ge(parts_out, b * PARTS_OUT)
                pool.sem_inc(stored, 1)
            pool.wait_ge(xn_ok, B)
            pool.wait_ge(mod_ok, 1)
            for b in range(B):
                xb = X[:, b * TB:(b + 1) * TB, :]
                g.tensor_tensor(xb, xb, gtmp[:, 0, b:b + 1, :].to_broadcast([P, TB, D]), ALU.add).then_inc(res_ok, 1)

            pool.wait_ge(slots_ok, 1)
            pool.wait_ge(zero_out, 16 * 8)
            for t in range(NT):
                g.indirect_dma_start(x_sorted, bass.IndirectOffsetOnAxis(ap=slot[:, t:t + 1], axis=0), XH[:, t, :], None)\
                    .then_inc(sorted_out, 16)
            for k in range(2):
                pool.wait_ge(y_out[k], (SLOT_TILES // 2 + 1) * 16)
            for t in range(NT):
                g.indirect_dma_start(YG[:, t, :], None, y_sorted, bass.IndirectOffsetOnAxis(ap=slot[:, t:t + 1], axis=0))\
                    .then_inc(gathered[t // TB], 16)

        @block.scalar
        def _(act):
            a = nc.scalar
            row = lambda v: v.rearrange("(a n) -> a n", a=1)
            for r0, src in ((0, b1.rearrange("e (c f) -> (e c) f", f=P)), (32, gamma), (40, beta), (48, cent), (56, c),
                            (60, row(bq)), (61, row(bk))):
                act.dma_start(rows[r0:r0 + src.shape[0], :], src).then_inc(rows_in, 16)
            act.dma_start(bv_b[:, :], row(bv).to_broadcast([P, D])).then_inc(bias_in, 16)
            act.dma_start(bo_b[:, :], row(bo).to_broadcast([P, D])).then_inc(bias_in, 16)
            act.dma_start(lam_c[:, :], row(lam).to_broadcast([P, 1])).then_inc(bias_in, 16)
            act.dma_start(b2_b[:, :], row(b2.rearrange("e d -> (e d)")).to_broadcast([P, E * D])).then_inc(bias_in, 16)
            act.wait_ge(cols_ok, 1)
            a.activation(silu[:, 0, :], cols[:, 56:60], ACT.Exp, scale=-1.0).then_inc(silu_e, 1)
            act.wait_ge(stats_ok, 1)
            a.activation(lnt[:, 6, :], lnt[:, 5, :], ACT.Sqrt).then_inc(root_ok, 1)
            act.wait_ge(modT_ok, 1)
            act.sem_inc(exp_ok, SB_)
            act.sem_inc(ot_ok, 1)
            for half in range(2):
                act.sem_inc(ot_out[half], 16)

            def tanh_q(b):
                act.wait_ge(q32_ok, b + 1)
                if not isinstance(b, int):
                    act.wait_ge(stored, b)
                a.activation(T32[:, 4, :], T32[:, 0, :], ACT.Tanh, scale=HD ** 0.5).then_inc(tanh_ok, 1)

            def first_q(b):
                a.activation(T16[:, 0, 0, :], T32[:, 0, :], ACT.Copy).then_inc(first_ok, 1)

            def tanh_k(b):
                act.wait_ge(k32_ok, b + 1)
                a.activation(T32[:, 2, :], T32[:, 1, :], ACT.Tanh)

            def first_tanh_k(b):
                a.activation(T16[:, 2, 0, :], T32[:, 1, :], ACT.Tanh).then_inc(first_ok, 1)

            def first_k(b):
                a.activation(T16[:, 1, 0, :], T32[:, 1, :], ACT.Copy).then_inc(first_ok, 1)

            def first_j(b):
                act.wait_ge(j32_ok, b + 1)
                a.activation(T16[:, 3, 0, :], T32[:, 3, :], ACT.Copy).then_inc(first_ok, 1)
            act_prep = {}
            for unit, steps in ((P_UNIT["Q"], (tanh_q, first_q)), (P_UNIT["K"], (tanh_k, first_tanh_k, first_k)),
                                (P_UNIT["J"], (first_j,))):
                for n, step in enumerate(steps):
                    act_prep.setdefault(unit + (n + 1) // 2, []).append((1 if n % 2 else 3, step))
            for step in (tanh_q, first_q, tanh_k, first_tanh_k, first_k, first_j):
                step(0)

            def evacuate(b, g, half):
                act.wait_ge(pv_ok, (b * NG + g) * NU + max(u for u in HALF_END if HALF_END[u] == half) + 1 + EB)
                act.wait_ge(ot_out[half], (b * NG + g + 1) * 16)
                a.activation(OT[:, half, :], PS[:, 7, :], ACT.Copy).then_inc(ot_ok, 1)

            def attention(b, last):
                for g in range(NG):
                    for u, (qc, kb) in enumerate(UNITS):
                        off = max(0, kb - 4 * qc) * P
                        for h in range(HG):
                            n = u * HG + h
                            act.wait_ge(s_ps, (b * NG + g) * NU * HG + n + 1)
                            if h == 0:
                                act.wait_ge(pv_ok, (b * NG + g) * NU + u + 1)
                            a.activation(PT[:, u % EB, h, off:HALF], PS[:, 4 + n % SB_, off:HALF], ACT.Exp).then_inc(exp_ok, 1)
                            for at, step in act_prep.get(u, ()):
                                if g == 0 and at == h and not last:
                                    step(b + 1)
                        if u == LAG + 3:
                            evacuate(b, g, 0)
                        if u == LAG - 1 and g:
                            evacuate(b, g - 1, 1)
                evacuate(b, NG - 1, 1)
            act.wait_ge(zero_out, 16 * 8)
            with act.Fori(0, B - 1) as b:
                attention(b, False)
            attention(B - 1, True)

            for k in range(16):
                act.wait_ge(w_tr, k + 1)
                dst = (W1T if k < 8 else W2T)[:, (k % 8) * HALF:(k % 8 + 1) * HALF]
                a.activation(dst, PS[:, 4 + k % 4, :], ACT.Copy).then_inc(w_ev, 1)
            for k in range(2):
                act.wait_ge(stats_ok, 2 + k)
                a.activation(lnt[:, 6, :], lnt[:, 5, :], ACT.Sqrt).then_inc(root_ok, 1)
                if k == 0:
                    for b in range(B):
                        act.wait_ge(h2t_ps, b + 1)
                        a.activation(AT[:, b * S:(b + 1) * S], ps2(2 * (b % 2)), ACT.Copy).then_inc(h2t_ok, 1)
            act.wait_ge(oh_ok, 1)
            a.activation(rs[:, 1, 0:NT], rs[:, 0, 0:NT], ACT.Exp, scale=-1.0).then_inc(alpha_e, 1)

            act.wait_ge(slots_ok, 1)
            act.sem_inc(xt_ok, 2)
            act.sem_inc(hr_ok, 2)
            for k in range(2):
                act.sem_inc(y_out[k], 16)

            def expert(n):
                return act.value_load(tile_e[0:1, bass.ds(n, 1)], min_val=0, max_val=E - 1)

            def scaled(n, j):
                e = expert(n)
                act.wait_ge(xsT_ps, n + 1 + 4)
                act.wait_ge(h_ps, n + 1)
                a.activation(XT[:, j % 2, :], PS[:, j % 2, 0:P], ACT.Identity, scale=cols[:, bass.ds(e + 32, 1)],
                             bias=cols[:, bass.ds(e + 40, 1)]).then_inc(xt_ok, 1)

            def hidden(n, j):
                e = expert(n)
                act.wait_ge(h_ps, n + 1 + 2)
                act.wait_ge(y_ps, n + 1)
                for k in range(FC):
                    last = a.activation(HR[:, j % 2, k * P:(k + 1) * P], PS[:, 4 + j % 2, k * P:(k + 1) * P], ACT.Relu,
                                        bias=cols[:, bass.ds(e * FC + k, 1)])
                last.then_inc(hr_ok, 1)

            def store_y(n, j):
                act.wait_ge(ys_ok, n + 1 + 2)
                act.dma_start(y_sorted[bass.ds(n * P, P), :], YS[:, j % 2, :]).then_inc(y_out[j % 2], 16)

            def act_step(n, j, first=False, tx=True):
                hidden(n, j)
                if tx:
                    scaled(n + 2, j)
                if not first:
                    store_y(n - 2, j)
            scaled(0, 0)
            scaled(1, 1)
            act_step(0, 0, first=True)
            act_step(1, 1, first=True)
            with act.Fori(0, (SLOT_TILES - 4) // 4) as i:
                for j in range(4):
                    act_step(i * 4 + 2 + j, j)
            for n in (SLOT_TILES - 2, SLOT_TILES - 1):
                act_step(n, n, tx=False)
            store_y(SLOT_TILES - 2, 0)
            store_y(SLOT_TILES - 1, 1)

        @block.tensor
        def _(pe):
            t_ = nc.tensor
            mm = t_.matmul
            pe.sem_inc(pv_ok, EB)
            pe.wait_ge(consts_ok, 1)
            pe.wait_ge(rows_in, 7 * 16)
            t_.transpose(PS[:, 0, 0:62], rows[0:62, :], ident[0:62, 0:62]).then_inc(cols_ps, 1)
            pe.wait_ge(w_in, 5 * 16)
            for n in range(4):
                last = t_.transpose(PS[:, 1, n * P:(n + 1) * P], wraw[:, n, :], ident[:, :])
            last.then_inc(wT_ps, 1)
            pe.wait_ge(silu_ok, 1)
            for k in range(2):
                mm(PS[:, 2, k * B:(k + 1) * B], wm[:, k * D:(k + 1) * D], silu[:, 3, :], start=(k == 0), stop=True,
                   skip_group_check=True)
            for b in range(B):
                last = mm(PS[:, 4 + b, :], silu_b[:, b, :], wm[:, 2 * D:6 * D], start=True, stop=True)
            last.then_inc(mod_ps, 1)
            pe.wait_ge(wT_ok, 1)
            pe.wait_ge(modT_ok, 1)

            def project(b, step, bank):
                halves = lambda w, src: [mm(PS[:, bank + k, :], w, src[:, k * HALF:(k + 1) * HALF], start=True, stop=True)
                                         for k in range(2)][-1]
                if step == "X":
                    pe.wait_ge(xn_ok, b + 1)
                    for t in range(TB):
                        last = t_.transpose(ps2(bank)[:, t * P:(t + 1) * P], XN[:, t, :], ident[:, :])
                elif step == "J":
                    pe.wait_ge(tanh_ok, b + 1)
                    last = halves(JL[:, :], T32[:, 4, :])
                else:
                    pe.wait_ge(ht_ok, b + 1)
                    if step in "QK":
                        last = halves(wT[:, "QK".index(step), :], HT)
                    else:
                        for t in range(4):
                            n = "V0 V1".split().index(step) * 4 + t
                            last = mm(PS[:, bank, t * P:(t + 1) * P], HT[:, n * P:(n + 1) * P], wT[:, 2, :], start=(t == 0),
                                      stop=True, skip_group_check=True)
                last.then_inc(max_ps, 1)

            def maximum(kind, g, k, index, slot_, loads, group):
                pe.wait_ge(max_used, index + 1)
                bank = 2 * slot_
                if kind == "P":
                    project(loads, PREP[k], bank)
                    return
                if kind == "T":
                    pe.wait_ge(m_parts_ok, group + 1)
                    t_.transpose(PS[:, bank, 0:P // 2].bitcast(BF16)[0:HG * 3 * TB, :],
                                 mparts[:, :, :, :].rearrange("p h j t -> p (h j t)"), identb[:, :]).then_inc(max_ps, 1)
                    return
                h, t = MTILES[k]
                if k == 0:
                    pe.wait_ge(stack_in[g], (loads + 1) * 10 * 16)
                n = (t + 1) * P
                for c0 in range(0, n, HALF):
                    c1 = min(n, c0 + HALF)
                    last = mm(PS[:, bank + c0 // HALF, 0:c1 - c0], SQ(g, h)[0:KROWS, t * P:(t + 1) * P],
                              SK(g, h)[0:KROWS, c0:c1], start=True, stop=True)
                last.then_inc(max_ps, 1)

            for i, (kind, ahead, k) in enumerate(FIRST):
                maximum(kind, ahead, k, i, i % MB_, 0, ahead)

            def products(b, g, u):
                qc, kb = UNITS[u]
                pe.wait_ge(exp_ok, ((b * NG + g) * NU + u + 1) * HG + SB_)
                if kb == 0:
                    pe.wait_ge(ot_ok, (b * NG + g) * 2 + qc + 1)
                off = max(0, kb - 4 * qc) * P
                for h in range(HG):
                    last = mm(PS[32 * h:32 * h + VW, 7, off:HALF],
                              Vs[:, g, (kb * HG + h) * VW:(kb * HG + h + 1) * VW], PT[:, u % EB, h, off:HALF],
                              start=(kb == 0), stop=(u in HALF_END), skip_group_check=True)
                last.then_inc(pv_ok, 1)

            pe.wait_ge(mod_ok, 1)

            def attention(b, b_last):
                trail = []
                for g in range(NG):
                    gi = b * NG + g
                    todo = (LAST_ITEMS if b_last else ITEMS)[g]
                    for u, (qc, kb) in enumerate(UNITS):
                        if u == 0:
                            pe.wait_ge(m_in, (gi + 1) * HG * 16)
                        off = max(0, kb - 4 * qc) * P
                        for h in range(HG):
                            n = u * HG + h
                            pe.wait_ge(exp_ok, gi * NU * HG + n + 1)
                            bank = PS[:, 4 + n % SB_, :]
                            last = mm(bank[:, off:HALF], SK(g, h)[0:MROWS, kb * P:(kb + 1) * P],
                                      SQ(g, h)[0:MROWS, qc * HALF + off:(qc + 1) * HALF], start=True, stop=True, skip_group_check=True)
                            if u in DIAG:
                                last = mm(bank[:, off:off + P], identb[:, :], after[:, :], start=False, stop=True,
                                          skip_group_check=True)
                            last.then_inc(s_ps, 1)
                            for i, _, kind, place, ahead, k in [it for it in todo if it[1] == n]:
                                maximum(kind, place, k, b * PER + N0 + i, (N0 + i) % MB_,
                                        b + 1 if kind == "P" else b + (g + ahead) // NG, gi + ahead)
                        trail.append((g, u))
                        if len(trail) > LAG:
                            products(b, *trail.pop(0))
                for g, u in trail:
                    products(b, g, u)
            with pe.Fori(0, B - 1) as b:
                attention(b, False)
            attention(B - 1, True)

            for b in range(B):
                pe.wait_ge(at_ok, b + 1)
                for t in range(TB):
                    n = b * TB + t
                    last = mm(ps2(2 * b)[:, t * P:(t + 1) * P], AT[:, n * P:(n + 1) * P], WOG[:, b, :], start=(t % 4 == 0),
                              stop=True, skip_group_check=True)
                last.then_inc(o_ps, 1)
            pe.wait_ge(w12_in, 32)
            pe.wait_ge(x1_ok, B)
            for k in range(16):
                if k >= 4:
                    pe.wait_ge(w_ev, k - 3)
                for j in range(4):
                    n = (k % 8) * 4 + j
                    last = t_.transpose(PS[:, 4 + k % 4, j * P:(j + 1) * P], (W1r if k < 8 else W2r)[:, n, :], ident[:, :])
                last.then_inc(w_tr, 1)
            for b in range(B):
                pe.wait_ge(h2_ok, b + 1)
                if b >= 2:
                    pe.wait_ge(h2t_ok, b - 1)
                for t in range(TB):
                    last = t_.transpose(ps2(2 * (b % 2))[:, t * P:(t + 1) * P], H2[:, b * TB + t, :], ident[:, :])
                last.then_inc(h2t_ps, 1)
            pe.wait_ge(w_ev, 16)
            for b in range(B):
                pe.wait_ge(h2t_ok, b + 1)
                for t in range(TB):
                    n = b * TB + t
                    last = mm(PS[:, 4, n * E:(n + 1) * E], AT[:, n * P:(n + 1) * P], cols[:, 48:56], start=(n == 0), stop=True,
                              skip_group_check=True)
            last.then_inc(score_ps, 1)
            pe.wait_ge(oh_ok, 2)
            mm(PS[:, 5, 0:NT * E], triu[:, :], ohb[:, :], start=True, stop=True)
            mm(PS[:, 6, 0:NT * E], onesb[:, :], ohb[:, :], start=True, stop=True).then_inc(cnt_ps, 1)
            pe.wait_ge(slots_ok, 1)
            pe.sem_inc(xsT_ps, 4)
            pe.sem_inc(h_ps, 2)
            pe.sem_inc(y_ps, 2)

            def expert(n):
                return pe.value_load(tile_e[0:1, bass.ds(n, 1)], min_val=0, max_val=E - 1)

            def turn(n, j, q=None):
                pe.wait_ge(xs_in[j % 4], ((n // 4 if q is None else q) + 1) * 16)
                pe.wait_ge(xt_ok, n + 1)
                t_.transpose(PS[:, j % 2, 0:P], XS[:, j % 4, :], ident[:, :]).then_inc(xsT_ps, 1)

            def up(n, j):
                pe.wait_ge(xt_ok, n + 1 + 2)
                pe.wait_ge(w1_ok, n + 1)
                pe.wait_ge(hr_ok, n + 1)
                for k in range(FC):
                    last = mm(PS[:, 4 + j % 2, k * P:(k + 1) * P], W1C[:, j % 2, k * P:(k + 1) * P], XT[:, j % 2, :],
                              start=(k == 0), stop=True, skip_group_check=True)
                last.then_inc(h_ps, 1)

            def down(n, j):
                e = expert(n)
                pe.wait_ge(hr_ok, n + 1 + 2)
                pe.wait_ge(ys_ok, n + 1)
                for k in range(FC):
                    last = mm(PS[:, 6 + j % 2, 0:D], HR[:, j % 2, k * P:(k + 1) * P],
                              W2T[:, bass.ds(e * FF + k * P, P)], start=(k == 0), stop=(k == FC - 1))
                last.then_inc(y_ps, 1)

            def pe_step(n, j, h=True, tx=True, q=None):
                if tx:
                    turn(n + 2, j + 2, q)
                if h:
                    up(n + 1, j + 1)
                down(n, j)
            turn(0, 0)
            turn(1, 1)
            up(0, 0)
            pe_step(0, 0)
            pe_step(1, 1)
            with pe.Fori(0, (SLOT_TILES - 4) // 4) as i:
                for j in range(4):
                    pe_step(i * 4 + 2 + j, j + 2, q=i + 1)
            pe_step(SLOT_TILES - 2, SLOT_TILES - 2, tx=False)
            pe_step(SLOT_TILES - 1, SLOT_TILES - 1, tx=False, h=False)

        @block.vector
        def _(dve):
            v = nc.vector
            count = [0]

            def link(ins):
                count[0] += 1
                ins.then_inc(dve_chain, 1)
                dve.wait_ge(dve_chain, count[0])

            def tt(o, a, b_, op):
                return v.tensor_tensor(o, a, b_, op)

            def statistics(src, rounds):
                with dve.Fori(0, B) as b:
                    for t in range(TB):
                        last = v.bn_stats(stat[:, bass.ds(b * TB + t, 1), :].rearrange("p a k -> p (a k)"),
                                          src[:, bass.ds(b * TB + t, 1), :].rearrange("p a d -> p (a d)"))
                    last.then_inc(bn_ok, 1)
                dve.wait_ge(bn_ok, B * rounds)
                L = lambda k: lnt[:, k, :]
                tt(L(0), stat[:, :, 1], stat[:, :, 4], ALU.add)
                tt(L(2), stat[:, :, 2], stat[:, :, 5], ALU.add)
                link(tt(L(1), stat[:, :, 1], stat[:, :, 4], ALU.subtract))
                v.tensor_scalar(L(0), L(0), 0.5, None, ALU.mult)
                link(tt(L(3), L(1), L(1), ALU.mult))
                link(v.scalar_tensor_tensor(L(4), L(3), D / 4.0, L(2), ALU.mult, ALU.add))
                v.tensor_scalar(L(5), L(4), 1.0 / D, EPS, ALU.mult, ALU.add).then_inc(stats_ok, 1)
                dve.wait_ge(root_ok, rounds)
                link(v.reciprocal(L(7), L(6)))
                link(tt(L(8), L(5), L(7), ALU.mult))
                link(tt(L(8), L(8), L(6), ALU.add))
                link(v.tensor_scalar(L(8), L(8), 0.5, None, ALU.mult))
                link(v.reciprocal(L(9), L(8)))

            def normed(o, src, n):
                return v.tensor_scalar(o, src[:, bass.ds(n, 1), :].rearrange("p a d -> p (a d)"), lnt[:, 0, bass.ds(n, 1)],
                                       lnt[:, 9, bass.ds(n, 1)], ALU.subtract, ALU.mult)

            dve.sem_inc(max_used, MB_)
            dve.wait_ge(cols_ps, 1)
            v.tensor_copy(cols[:, 0:62], PS[:, 0, 0:62]).then_inc(cols_ok, 1)
            dve.wait_ge(cols_ok, 1)
            v.tensor_scalar(bqs[:, :], cols[:, 60:61], HD ** -0.5, None, ALU.mult)
            dve.wait_ge(silu_e, 1)
            link(v.tensor_scalar(silu[:, 1, :], silu[:, 0, :], 1.0, None, ALU.add))
            link(v.reciprocal(silu[:, 2, :], silu[:, 1, :]))
            link(tt(silu[:, 3, :], silu[:, 2, :], cols[:, 56:60], ALU.mult))
            v.tensor_copy(silu_b[:, :, :], silu[:, 3, :].unsqueeze(2).to_broadcast([P, B, P])).then_inc(silu_ok, 1)
            dve.wait_ge(wT_ps, 1)
            v.tensor_copy(wT[:, :, :].rearrange("p n d -> p (n d)"), PS[:, 1, :]).then_inc(wT_ok, 1)
            for b in range(B):
                dve.wait_ge(x_in[b], 16)
            statistics(X, 1)
            dve.wait_ge(j_in, H * 16)
            dve.wait_ge(bias_in, 4 * 16)
            v.tensor_scalar(JL[:, :], JB[:, :], lam_c[:, :], None, ALU.mult)
            dve.wait_ge(mod_ps, 1)
            dve.wait_ge(wT_ok, 1)
            v.tensor_copy(modT[:, 0, :], PS[:, 2, 0:B])
            v.tensor_scalar(modT[:, 1, :], PS[:, 2, B:2 * B], 1.0, None, ALU.add).then_inc(modT_ok, 1)
            dve.wait_ge(modT_ok, 1)

            def conditioning():
                link(v.tensor_copy(MB[:, :, :, :].rearrange("p b k d -> p b (k d)"), PS[:, 4:8, :]))
                v.tensor_scalar(MB[:, :, 2, :], MB[:, :, 2, :], 1.0, None, ALU.add)
                for k in (0, 3):
                    gate, sign, size = MB[:, :, k, :], gtmp[:, 0, :, :], gtmp[:, 1, :, :]
                    link(v.tensor_scalar(sign, gate, 0.0, 2.0, ALU.is_ge, ALU.mult))
                    v.scalar_tensor_tensor(size, gate, -1.0, gate, ALU.mult, ALU.max)
                    link(v.tensor_scalar(sign, sign, 1.0, None, ALU.subtract))
                    link(v.scalar_tensor_tensor(gate, size, 0.25, sign, ALU.max, ALU.mult))
                tt(WOG[:, :, :], MB[:, :, 0, :], wT[:, 3:4, :].to_broadcast([P, B, D]), ALU.mult)
                tt(gtmp[:, 0, :, :], MB[:, :, 0, :], bo_b[:, :].unsqueeze(1).to_broadcast([P, B, D]), ALU.mult).then_inc(mod_ok, 1)
                dve.wait_ge(mod_ok, 1)

            def norm_row(b, t):
                if t == 0 and not isinstance(b, int):
                    dve.wait_ge(stored, b)
                last = normed(XN[:, t, :], X, b * TB + t)
                if t == TB - 1:
                    last.then_inc(xn_ok, 1)

            def projected(b, step, bank):
                src = ps2(bank)
                later = not isinstance(b, int)
                if step == "X":
                    v.tensor_scalar(HT[:, :], src, modT[:, 1, bass.ds(b, 1)], modT[:, 0, bass.ds(b, 1)], ALU.mult, ALU.add)\
                        .then_inc(max_used, 1)
                elif step == "Q":
                    v.tensor_scalar(T32[:, 0, :], src, HD ** -0.5, bqs[:, :], ALU.mult, ALU.add).then_inc(max_used, 1)
                elif step == "K":
                    v.tensor_scalar(T32[:, 1, :], src, cols[:, 61:62], None, ALU.add).then_inc(max_used, 1)
                elif step == "J":
                    v.tensor_copy(T32[:, 3, :], src).then_inc(max_used, 1)
                else:
                    half = "V0 V1".split().index(step)
                    if later and half == 0:
                        for g in range(NG):
                            dve.wait_ge(stack_in[g], b * 10 * 16)
                    for g in range(NG):
                        last = tt(VA[:, g, half * 4:half * 4 + 4, :, 0:HD],
                                  src[:, 0:HALF].rearrange("p (t g h w) -> p g t h w", t=4, g=NG, h=HG)[:, g],
                                  bv_b[:, g * HG * HD:(g + 1) * HG * HD].rearrange("p (h w) -> p h w", h=HG).unsqueeze(1)
                                  .to_broadcast([P, 4, HG, HD]), ALU.add)
                    last.then_inc(max_used, 1)

            def maximum(kind, place, k, index, slot_, group):
                dve.wait_ge(max_ps, index + 1)
                bank = 2 * slot_
                if kind == "P":
                    projected(group, PREP[k], bank)
                    signal = dict(X=ht_ok, Q=q32_ok, K=k32_ok, J=j32_ok, V1=va_ok).get(PREP[k])
                    if signal is not None:
                        dve.wait_ge(max_used, index + 1 + MB_)
                        dve.sem_inc(signal, 1)
                    return
                if kind == "T":
                    if not (isinstance(group, int) and group == 0):
                        dve.wait_ge(m_in, group * HG * 16)
                    v.tensor_copy(mrow[:, :], PS[:, bank, 0:P // 2].bitcast(BF16)[0:HG * 3 * TB, :]).then_inc(max_used, 1)
                    return
                h, t = MTILES[k]
                n = (t + 1) * P
                src = ps2(bank)[:, 0:n]
                dve.sem_inc(max_seen, 1)
                v.tensor_tensor_reduce(out=src, in0=src, in1=mask[:, S - n:S], scale=1.0, scalar=-3e38, op0=ALU.add, op1=ALU.max,
                                       accum_out=maxima[:, place, h * TB + t:h * TB + t + 1]).then_inc(max_used, 1)
                if k == NM - 1:
                    m = maxima[:, place, :].rearrange("p (h t) -> p h t", h=HG)
                    rest = mres[:, 0, :].rearrange("p (h t) -> p h t", h=HG)
                    dve.wait_ge(max_used, index + 1 + MB_)
                    for step, ins in enumerate((
                            lambda: v.tensor_scalar(mparts[:, :, 0, :], m, -1.0, None, ALU.mult),
                            lambda: v.scalar_tensor_tensor(rest, m, -1.0, mparts[:, :, 0, :], ALU.mult, ALU.subtract),
                            lambda: v.tensor_copy(mparts[:, :, 1, :], rest))):
                        ins().then_inc(m_split, 1)
                        dve.wait_ge(m_split, group * 3 + step + 1)
                    tt(mparts[:, :, 2, :], rest, mparts[:, :, 1, :], ALU.subtract).then_inc(m_parts_ok, 1)

            for t in range(TB):
                norm_row(0, t)
            def split0(n):
                k = TENSORS[n][0]
                dve.wait_ge(first_ok, n + 1)
                a = T32[:, k, :]
                steps = 2 * (n - 1)
                tt(a, a, T16[:, k, 0, :], ALU.subtract).then_inc(split0_step, 1)
                dve.wait_ge(split0_step, steps + 1)
                v.tensor_copy(T16[:, k, 1, :], a).then_inc(split0_step, 1)
                dve.wait_ge(split0_step, steps + 2)
                tt(T16[:, k, 2, :], a, T16[:, k, 1, :], ALU.subtract).then_inc(split0_ok, 1)

            for i, (kind, ahead, k) in enumerate(FIRST):
                maximum(kind, ahead, k, i, i % MB_, ahead)
                if i == len(PREP) - 1:
                    for n in range(1, 4):
                        split0(n)
                    conditioning()

            def attention(b, b_last):
                for g in range(NG):
                    for n, (i, _, kind, place, ahead, k) in enumerate((LAST_ITEMS if b_last else ITEMS)[g]):
                        maximum(kind, place, k, b * PER + N0 + i, (N0 + i) % MB_, b + 1 if kind == "P" else b * NG + g + ahead)
                        if g == 0 and n < TB and not b_last:
                            norm_row(b + 1, n)
            with dve.Fori(0, B - 1) as b:
                attention(b, False)
            attention(B - 1, True)

            dve.wait_ge(num_in, 2 * B * 16)
            for b in range(B):
                part = slice(b * S, (b + 1) * S)
                link(v.reciprocal(DEN[:, part], DEN[:, part]))
                tt(AT[:, part], NUM[:, part], DEN[:, part], ALU.mult).then_inc(at_ok, 1)
            dve.wait_ge(res_ok, B)
            flat = lambda r: r.rearrange("p t d -> p (t d)")
            tiles = lambda b: slice(b * TB, (b + 1) * TB)
            for b in range(B):
                dve.wait_ge(o_ps, b + 1)
                xb = flat(X[:, tiles(b), :])
                tt(xb, xb, ps2(2 * b), ALU.add).then_inc(x1_ok, 1)
            dve.wait_ge(x1_ok, B)
            dve.wait_ge(at_ok, B)
            statistics(X, 2)
            over = lambda b, k: MB[:, b, k:k + 1, :].to_broadcast([P, TB, D])
            for b in range(B):
                for t in range(TB):
                    n = b * TB + t
                    last = normed(H2[:, n, :], X, n)
                link(last)
                hb = H2[:, tiles(b), :]
                link(tt(hb, hb, over(b, 2), ALU.mult))
                tt(hb, hb, over(b, 1), ALU.add).then_inc(h2_ok, 1)
            dve.wait_ge(h2_ok, B)
            statistics(H2, 3)
            for n in range(NT):
                last = normed(XH[:, n, :], H2, n)
            link(last)

            dve.wait_ge(score_ps, 1)
            link(v.tensor_copy(sc[:, :, :].rearrange("p t e -> p (t e)"), PS[:, 4, 0:NT * E]))
            best, idx = rs[:, 0, 0:NT], rs[:, 2, 0:NT]
            col = lambda r: r.unsqueeze(2).to_broadcast([P, NT, E])
            link(v.tensor_reduce(best, sc[:, :, :], AX.X, ALU.max))
            link(tt(rt[:, 0, :, :], sc[:, :, :], col(best), ALU.is_ge))
            link(v.scalar_tensor_tensor(rt[:, 1, :, :], rt[:, 0, :, :], -float(E), iota_e[:, :].unsqueeze(1).to_broadcast([P, NT, E]),
                                        ALU.mult, ALU.add))
            link(v.tensor_reduce(idx, rt[:, 1, :, :], AX.X, ALU.min))
            onehot = rt[:, 2, :, :]
            link(tt(onehot, rt[:, 1, :, :], col(idx), ALU.is_equal))
            dve.sem_inc(oh_ok, 1)
            v.tensor_copy(ohb[:, :], onehot.rearrange("p t e -> p (t e)")).then_inc(oh_ok, 1)
            dve.wait_ge(alpha_e, 1)
            link(v.tensor_scalar(rs[:, 3, 0:NT], rs[:, 1, 0:NT], 1.0, None, ALU.add))
            link(v.reciprocal(rs[:, 4, 0:NT], rs[:, 3, 0:NT]))
            alpha = rs[:, 4, :]
            dve.wait_ge(cnt_ps, 1)
            within = PS[:, 5, 0:NT * E].rearrange("p (t e) -> p t e", e=E)
            link(v.tensor_copy(rt[:, 3, :, :].rearrange("p t e -> p (t e)"), PS[:, 6, 0:NT * E]))
            v.memset(rs[:, 5, :], 1.0)
            link(v.memset(rt[:, 6, :, :], 0.0))
            for e in range(E):
                last = v.tensor_tensor_scan(rt[:, 4, :, e], rs[:, 5, 0:NT], rt[:, 3, :, e], 0.0, ALU.mult, ALU.add)
            link(last)
            few = rt[:, 6, :, :].rearrange("p t e -> p (t e)")
            link(tt(rt[:, 5, :, :].rearrange("p t e -> p (t e)").rearrange("p (e t) -> p e t", e=E),
                    rt[:, 4, NT - 1, :].unsqueeze(2).to_broadcast([P, E, NT]),
                    iota_n[:, :].unsqueeze(1).to_broadcast([P, E, NT]), ALU.is_gt))
            link(v.tensor_reduce(few[:, 0:E], rt[:, 5, :, :].rearrange("p t e -> p (t e)").rearrange("p (e t) -> p e t", e=E), AX.X, ALU.add))
            link(v.tensor_tensor_scan(few[:, E:2 * E], rs[:, 5, 0:E], few[:, 0:E], 0.0, ALU.mult, ALU.add))
            link(tt(few[:, 2 * E:3 * E], few[:, E:2 * E], few[:, 0:E], ALU.subtract))
            link(tt(rt[:, 4, :, :], rt[:, 4, :, :], rt[:, 3, :, :], ALU.subtract))
            link(tt(rt[:, 4, :, :], rt[:, 4, :, :], within, ALU.add))
            link(v.scalar_tensor_tensor(rt[:, 4, :, :], few[:, 2 * E:3 * E].unsqueeze(1).to_broadcast([P, NT, E]), float(P),
                                        rt[:, 4, :, :], ALU.mult, ALU.add))
            link(tt(rt[:, 4, :, :], rt[:, 4, :, :], onehot, ALU.mult))
            link(v.tensor_reduce(rs[:, 6, 0:NT], rt[:, 4, :, :], AX.X, ALU.add))
            v.tensor_copy(slot[:, :], rs[:, 6, 0:NT])
            cmp_ = rt[:, 7, :, :].rearrange("p t e -> p (t e)")
            ne = E - 1
            for t0 in range(0, SLOT_TILES, 20):
                link(tt(cmp_[:, 0:20 * ne].rearrange("p (t e) -> p t e", e=ne),
                        few[:, E:2 * E - 1].unsqueeze(1).to_broadcast([P, 20, ne]),
                        iota_t[:, t0:t0 + 20].unsqueeze(2).to_broadcast([P, 20, ne]), ALU.is_le))
                link(v.tensor_reduce(rs[:, 7, t0:t0 + 20], cmp_[:, 0:20 * ne].rearrange("p (t e) -> p t e", e=ne), AX.X, ALU.add))
            v.tensor_copy(tile_e[:, :], rs[:, 7, :]).then_inc(slots_ok, 1)

            dve.wait_ge(slots_ok, 1)
            dve.sem_inc(ys_ok, 2)

            def copy_w1(n, j):
                e = dve.value_load(tile_e[0:1, bass.ds(n, 1)], min_val=0, max_val=E - 1)
                dve.wait_ge(h_ps, n + 1)
                v.tensor_copy(W1C[:, j % 2, :], W1T[:, bass.ds(e * FF, FF)]).then_inc(w1_ok, 1)

            def biased(n, j, q=None):
                e = dve.value_load(tile_e[0:1, bass.ds(n, 1)], min_val=0, max_val=E - 1)
                dve.wait_ge(y_ps, n + 1 + 2)
                dve.wait_ge(y_out[j % 2], ((n // 2 if q is None else q) + 1) * 16)
                tt(YS[:, j % 2, :], PS[:, 6 + j % 2, 0:D], b2_b[:, bass.ds(e * D, D)], ALU.add).then_inc(ys_ok, 1)
            copy_w1(0, 0)
            copy_w1(1, 1)
            with dve.Fori(0, (SLOT_TILES - 4) // 4) as i:
                for j in range(4):
                    copy_w1(i * 4 + 2 + j, j)
                    biased(i * 4 + j, j, i * 2 + j // 2)
            for n in range(SLOT_TILES - 4, SLOT_TILES):
                if n + 2 < SLOT_TILES:
                    copy_w1(n + 2, n)
                biased(n, n)

            for b in range(B):
                dve.wait_ge(gathered[b], TB * 16)
                for t in range(TB):
                    n = b * TB + t
                    last = v.scalar_tensor_tensor(YG[:, n, :], YG[:, n, :], alpha[:, n:n + 1], H2[:, n, :], ALU.mult, ALU.add)
                link(last)
                yb = YG[:, tiles(b), :]
                link(tt(yb, yb, over(b, 3), ALU.mult))
                tt(yb, yb, X[:, tiles(b), :], ALU.add).then_inc(fin_ok, 1)


_INS = ['L0_attn_x', 'L0_attn_Wq', 'L0_attn_bq', 'L0_attn_Wk', 'L0_attn_bk', 'L0_attn_Wv', 'L0_attn_bv', 'L0_attn_Wo',
        'L0_attn_bo', 'L0_attn_J_attn', 'L0_attn_lambda_attn', 'L0_ffn_centroids', 'L0_ffn_gamma', 'L0_ffn_beta',
        'L0_ffn_W1', 'L0_ffn_b1', 'L0_ffn_W2', 'L0_ffn_b2', 'L0_c', 'L0_wmod']
_OUTS = [((B, S, D), 'float32')]


def kernel(**inputs):
    import numpy as _np
    import concourse.bacc as _bacc
    from concourse import mybir as _mybir
    from concourse.bass_utils import run_bass_kernel_spmd as _run

    nc = _bacc.Bacc("TRN2", target_bir_lowering=False, num_devices=1)
    arrays, args = {}, []
    for name in _INS:
        a = _np.ascontiguousarray(inputs[name])
        if a.ndim == 0:
            a = a.reshape(1)
        arrays[f"in_{name}_dram"] = a
        args.append(nc.dram_tensor(f"in_{name}_dram", a.shape, _mybir.dt.from_np(a.dtype), kind="ExternalInput").ap())
    for i, (shape, dtype) in enumerate(_OUTS):
        dt = _mybir.dt.from_np(_np.dtype(dtype))
        args.append(nc.dram_tensor(f"out_{i}_dram", shape, dt, kind="ExternalOutput").ap())
    build(nc, *args)
    r = _run(nc, [arrays], core_ids=[0])
    got = tuple(r.results[0][f"out_{i}_dram"] for i in range(len(_OUTS)))
    return got[0]
```

```python
import concourse.bass as bass
from concourse import mybir
from contextlib import ExitStack

F32 = mybir.dt.float32
BF16 = mybir.dt.bfloat16
I32 = mybir.dt.int32
ALU = mybir.AluOpType
ACT = mybir.ActivationFunctionType
AX = mybir.AxisListType

B, S, D = 4, 1024, 128
H, HD = 16, 8
E, FF = 8, 512
P = 128
TB = S // P
NT = B * TB
HG = 4
NG = H // HG
GROUPS = B * NG
HALF = 512
EPS = 1e-5
BIG = 1e30
FC = FF // P
SLOT_TILES = (B * S + E * (P - 1)) // P + 1
assert SLOT_TILES == 40
ROW = 2 * HD
TERMS = 6
KROWS = ROW * TERMS
MROWS = KROWS + 3
VW = HD + 1
ROWW = 3 * D + 1
REG = B * S + P
U = 8
assert SLOT_TILES % U == 0


def build(nc, x, Wq, bq, Wk, bk, Wv, bv, Wo, bo, J, lam, cent, gamma, beta, W1, b1, W2, b2, c, wmod, out):
    ctx = ExitStack()
    with ctx:
        def sb(name, shape, dt=F32):
            return ctx.enter_context(nc.sbuf_tensor(name, shape, dt))

        def sem(name):
            return ctx.enter_context(nc.semaphore(name))

        def dram(name, shape, dt=F32):
            return nc.dram_tensor(name, shape, dt, kind="Internal").ap()

        q_parts = dram("q_parts", [B, H, 3, ROW, S], BF16)
        k_parts = dram("k_parts", [B, H, 3, ROW, S], BF16)
        o_raw = dram("o_raw", [B, NG, P, S])
        r_den = dram("r_den", [B, H, S])
        by_expert = dram("by_expert", [E * REG, ROWW])

        X = sb("X", [P, NT, D])
        ident = sb("ident", [P, P])
        identb = sb("identb", [P, P], BF16)
        mask = sb("mask", [P, S])
        wT = sb("wT", [P, 4, D])
        rows = sb("rows", [64, D])
        cols = sb("cols", [P, 64])
        JB = sb("JB", [P, P])
        JL = sb("JL", [P, P])
        lam_c = sb("lam_c", [P, 1])
        bqs = sb("bqs", [P, 1])
        bv_b = sb("bv_b", [P, D])
        bo_b = sb("bo_b", [P, D])
        silu = sb("silu", [P, 4, B])
        modT = sb("modT", [P, 2, B])
        MB = sb("MB", [P, B, 4, D])
        ga_bo = sb("ga_bo", [P, B, D])
        stat = sb("stat", [P, NT, 6])
        lnt = sb("lnt", [P, 8, NT])
        stat2 = sb("stat2", [P, TB, 6])
        ln2 = sb("ln2", [P, 8, TB])
        maxima = sb("maxima", [P, NG, HG * TB])
        mres = sb("mres", [P, 2, HG * TB])
        mparts = sb("mparts", [P, HG, 3, TB], BF16)
        mrow = sb("mrow", [HG * 3 * TB, P], BF16)
        HT = sb("HT", [P, S])
        OT = sb("OT", [P, 2, HALF])
        Vs = sb("Vs", [P, NG, TB * HG * VW])
        b2_b = sb("b2_b", [P, E * D])
        arenaA = sb("arenaA", [P, 24576])
        arenaB = sb("arenaB", [P, 12544])
        Aap = arenaA[:, :]
        Bap = arenaB[:, :]
        stacks = Aap[:, 0:16384].bitcast(BF16).rearrange("p (r s h q) -> p r s h q", r=4, s=2, h=HG)
        SQ = lambda r, h: stacks[:, r, 0, h, :]
        SK = lambda r, h: stacks[:, r, 1, h, :]
        PT = Aap[:, 16384:24576].rearrange("p (r h q) -> p r h q", r=4, h=HG)
        wraw = Aap[:, 16384:16896].rearrange("p (n d) -> p n d", n=4)
        silu_b = Aap[:, 16896:17408].rearrange("p (b d) -> p b d", b=B)
        wm = Aap[:, 17408:18176]
        W1r = Aap[:, 0:4096].rearrange("p (k d) -> p k d", d=D)
        W2r = Aap[:, 4096:8192].rearrange("p (k d) -> p k d", d=D)
        W1T = Aap[:, 8192:12288]
        W2T = Aap[:, 12288:16384]
        FB = 16384
        XS = Aap[:, FB:FB + U * ROWW].rearrange("p (r d) -> p r d", r=U)
        XSI = Aap[:, FB:FB + U * ROWW].bitcast(I32).rearrange("p (r d) -> p r d", r=U)
        FB += U * ROWW
        XT = Aap[:, FB:FB + 256].rearrange("p (r d) -> p r d", r=2)
        W1C = Aap[:, FB + 256:FB + 1280].rearrange("p (r d) -> p r d", r=2)
        HR = Aap[:, FB + 1280:FB + 2304].rearrange("p (r d) -> p r d", r=2)
        YS = Aap[:, FB + 2304:FB + 2560].rearrange("p (r d) -> p r d", r=2)
        B1C = Aap[:, FB + 2560:FB + 2560 + 4 * FC].rearrange("p (r d) -> p r d", r=4)
        T32 = Bap[:, 0:5120].rearrange("p (k s) -> p k s", k=5)
        T16 = Bap[:, 5120:11264].bitcast(BF16).rearrange("p (k j s) -> p k j s", k=4, j=3)
        VA = Bap[:, 11264:11264 + TB * H * VW].rearrange("p (g t h w) -> p g t h w", g=NG, t=TB, h=HG)
        XN = T32[:, 3, :].rearrange("p (t d) -> p t d", d=D)
        NUM, DEN, AT, H2f = (T32[:, k, :] for k in range(4))
        H2 = H2f.rearrange("p (t d) -> p t d", d=D)
        PAY = Bap[:, 5120:5120 + TB * ROWW].rearrange("p (t w) -> p t w", w=ROWW)
        PAYI = Bap[:, 5120:5120 + TB * ROWW].bitcast(I32).rearrange("p (t w) -> p t w", w=ROWW)
        WOG = sb("WOG", [P, B, D])
        triu = sb("triu", [P, P], BF16)
        onesb = sb("onesb", [P, P], BF16)
        after = sb("after", [P, P], BF16)
        iotai = sb("iotai", [P, 96], I32)
        iota_f = sb("iota_f", [P, 96])
        iota_e, iota_t, iota_n = iota_f[:, 0:E], iota_f[:, 0:SLOT_TILES], iota_f[:, 40:40 + NT + 1]
        token = sb("token", [P, NT], I32)
        DENP = sb("DENP", [P, P])
        rt = sb("rt", [P, 4, TB, E])
        rs = sb("rs", [P, 4, TB])
        ohb = sb("ohb", [P, TB * E], BF16)
        base = sb("base", [P, E])
        few = sb("few", [P, E])
        slot = sb("slot", [P, TB], I32)
        pad_slot = sb("pad_slot", [P, E], I32)
        pad_row = sb("pad_row", [P, ROWW])
        b1p = sb("b1p", [P, E * FC])
        tile_e = sb("tile_e", [P, SLOT_TILES], I32)
        tile_row = Bap[:, 1300:1300 + SLOT_TILES].bitcast(I32)
        tw = Bap[:, 0:E * (NT + 1)].rearrange("p (e t) -> p e t", e=E)
        tv = Bap[:, 512:512 + SLOT_TILES * (E - 1)].rearrange("p (t e) -> p t e", e=E - 1)
        tu = Bap[:, 800:800 + SLOT_TILES * (E - 1)].rearrange("p (t e) -> p t e", e=E - 1)
        ts = Bap[:, 1100:1300].rearrange("p (k t) -> p k t", k=5)
        PS = ctx.enter_context(nc.psum_tensor("PS", [P, 8, HALF], F32))

        ps2 = lambda k: PS[:, k:k + 2, :].rearrange("p a b -> p (a b)")

        (w_in, rows_in, bias_in, j_in, consts_ok, pool_chain, dve_chain, post_chain, cols_ps, cols_ok, 
         silu_e, silu_ok, mod_ps, mod_ok, modT_ok, wT_ps, wT_ok, xn_ok, ht_ok, q32_ok, tanh_ok, k32_ok, 
         j32_ok, first_ok, split_step, split_ok, split0_q, split0_step, split0_ok, parts0_out, pool_turn, 
         parts_out, stored, va_ok, max_ps, max_used, dve_turn, m_split, m_parts_ok, m_in, s_ps, exp_ok, 
         pv_ok, ot_ok, res_ok, bn_ok, den_in, den_ok, rden_out, num_in, at_ok, h2_ok, h2t_ok, best_ok, 
         alpha_t, alpha_ok, pay_ok, oh_ok, slots_ok, pool_step, sorted_out, sent, pads_ok, w12_in, w_tr, w_ev, b1_ps, 
         tiles_ok, xsT_ps, xt_ok, w1_ok, h_ps, hr_ok, y_ps, ys_step, ys_ok, sp_turn, pads_out, ones_ok, route_chain) = [sem(n) for n in (
            "w_in rows_in bias_in j_in consts_ok pool_chain dve_chain post_chain cols_ps cols_ok silu_e silu_ok "
            "mod_ps mod_ok modT_ok wT_ps wT_ok xn_ok ht_ok q32_ok tanh_ok k32_ok j32_ok first_ok split_step "
            "split_ok split0_q split0_step split0_ok parts0_out pool_turn parts_out stored va_ok max_ps "
            "max_used dve_turn m_split m_parts_ok m_in s_ps exp_ok pv_ok ot_ok res_ok bn_ok den_in den_ok "
            "rden_out num_in at_ok h2_ok h2t_ok best_ok alpha_t alpha_ok pay_ok oh_ok slots_ok pool_step sorted_out sent "
            "pads_ok w12_in w_tr w_ev b1_ps tiles_ok xsT_ps xt_ok w1_ok h_ps hr_ok y_ps ys_step ys_ok sp_turn pads_out ones_ok route_chain").split()]

        stack_in = [sem(f"stack_in{g}") for g in range(NG)]
        x_in = [sem(f"x_in{b}") for b in range(B)]
        ot_out = [sem(f"ot_out{k}") for k in range(2)]
        xs_in = [sem(f"xs_in{k}") for k in range(U)]
        y_out = [sem(f"y_out{k}") for k in range(2)]

        block = ctx.enter_context(nc.Block())

        UNITS = [(qc, kb) for qc in range(2) for kb in range(4 * qc + 4)]
        NU = len(UNITS)
        DIAG = [u for u, (qc, kb) in enumerate(UNITS) if kb >= 4 * qc]
        HALF_END = {max(u for u, (qc, _) in enumerate(UNITS) if qc == q): q for q in range(2)}
        LAG = 2
        SB_, EB, MB_ = 3, 4, 2
        MTILES = [(h, t) for h in range(HG) for t in (4, 0, 1, 5, 2, 3, 6, 7)]
        NM = len(MTILES)
        EARLY = 8
        SEQ = [("m", 1, k) for k in range(EARLY, NM)] + [("m", 2, 0), ("m", 2, 1), ("T", 1, 0)] + \
              [("m", 2, k) for k in range(2, EARLY)]
        PREP = ("X0", "X1", "Q0", "Q1", "K0", "K1", "V0", "V1", "J0", "J1")
        PREP_AT = tuple(9 + 2 * k for k in range(len(PREP)))
        FIRST = [("P", 0, k) for k in range(len(PREP))] + [("m", 0, k) for k in range(NM)] + \
                [("m", 1, 0), ("m", 1, 1), ("T", 0, 0)] + [("m", 1, k) for k in range(2, EARLY)]

        SLOT_COST = [70 * (kb >= 4 * qc) + (HALF - max(0, kb - 4 * qc) * P) * 0.87 for qc, kb in UNITS for h in range(HG)]

        POST = ("O0", "O1", "H0", "H1", "S", "C")
        LEAD = -1400
        NEWTON = 3
        MOMENTS = 6 + 3 * NEWTON
        root = lambda name, n0, at, n1=MOMENTS: tuple((at + (n - n0) // 2, "D", (name, n)) for n in range(n0, n1))
        ATT = 6
        POST_AT = {0: ((24, "D", "denominators"),),
                   2: ((ATT, "D", "attended"), (ATT + 2, "R", "O0"), (ATT + 3, "D", "stats_x0"), (ATT + 4, "R", "O1"),
                       (ATT + 5, "D", "stats_x1")) + root("root_x", 0, ATT + 6) +
                      ((ATT + 14, "D", "norm_x0"), (ATT + 15, "D", "norm_x1"), (ATT + 16, "D", "scale_h"), (ATT + 17, "D", "shift_h"),
                       (ATT + 19, "R", "H0"), (ATT + 19, "D", "stats_h0"), (ATT + 20, "R", "H1"), (ATT + 21, "D", "stats_h1")) +
                      root("root_h", 0, ATT + 22, 6) + ((ATT + 25, "R", "S"),),
                   3: tuple(it for n in range(6) for it in ((n, "D", ("best", n)), (n, "D", ("root_h", 6 + n)))) +
                      root("root_h", 12, 6) + ((8, "D", "norm_h0"), (8, "D", "weigh"), (9, "R", "C"), (10, "D", "norm_h1")) +
                      tuple((11 + n, "D", ("place", n)) for n in range(3))}
        D_COST = dict(denominators=870, attended=1090, stats_x0=800, stats_x1=800, norm_x0=800, norm_x1=800, scale_h=1090,
                      shift_h=1090, stats_h0=800, stats_h1=800, norm_h0=800, norm_h1=800, weigh=80)
        R_COST = dict(O0=(580, 872), O1=(580, 872), H0=(580, 548), H1=(580, 548), S=(130, 640), C=(300, 500))
        P_COST = dict(X=(580, 548), Q=(580, 858), K=(580, 858), V=(770, 872), J=(580, 858))

        def item_cost(g, n, kind, k, prep):
            dve, pe_ = (D_COST.get(k, 110), 0) if kind == "D" else R_COST[k] if kind == "R" else P_COST[PREP[k][0]] if kind == "P" else \
                (200, 70) if kind == "T" else (70 + (MTILES[k][1] + 1) * P + (500 if k == NM - 1 else 0), (MTILES[k][1] + 1) * 54)
            return dve + (200 if prep and g == 0 and n < TB else 0), pe_

        def schedule(prep, post, last):
            groups, n = [], 0
            for g in range(NG):
                seq = list(SEQ)
                extra = [(at, "P", k) for k, at in enumerate(PREP_AT)] if g == 0 and prep else []
                extra += POST_AT.get(g, ()) if post else ()
                for at, kind, k in reversed(sorted(extra, key=lambda it: it[0])):
                    seq.insert(at, (kind, 0, k))
                seq = [it for it in seq if not last or g + it[1] < NG]
                cost = [item_cost(g, m, kind, k, prep) for m, (kind, _, k) in enumerate(seq)]
                pace = (sum(SLOT_COST) + sum(c[1] for c in cost)) / max(1, sum(c[0] for c in cost))
                slots, clock, m = [], 0, 0
                for i in range(NU * HG):
                    clock += SLOT_COST[i]
                    while m < len(seq) and (sum(c[0] for c in cost[:m]) * pace <= clock + LEAD or i == NU * HG - 1):
                        clock += cost[m][1]
                        slots.append(i)
                        m += 1
                items = []
                for m, (kind, ahead, k) in enumerate(seq):
                    items.append((n, slots[m], kind, (g + ahead) % NG, ahead, k))
                    n += kind != "D"
                groups.append(items)
            return groups, n
        BODIES = dict(first=schedule(True, False, False), middle=schedule(True, True, False), last=schedule(False, True, True))
        N0 = len(FIRST)
        PER = BODIES["middle"][1]
        N1 = N0 + BODIES["first"][1]
        N_END = N1 + (B - 2) * PER + BODIES["last"][1]

        def use(body, b, i):
            return N0 + i if body == "first" else N1 + (b - 1) * PER + i

        def banks(seq):
            at, had, out_ = 0, [None] * 4, []
            for i, (kind, k) in enumerate(seq):
                wide = 2 if kind == "m" and MTILES[k][1] >= 4 or k == "C" else 1
                at += at % wide
                mine = [(at + w) % 4 for w in range(wide)]
                before = [had[m] for m in mine if had[m] is not None]
                out_.append((mine[0], max(before) if before else None))
                for m in mine:
                    had[m] = i
                at += wide
            return out_
        BANKS = {body: banks([(it[2], it[5]) for items in groups for it in items if it[2] != "D"])
                 for body, (groups, _) in BODIES.items()}
        FIRST_BANKS = banks([(kind, k) for kind, _, k in FIRST])
        TAIL_BANKS = banks([("R", k) for k in POST])

        def freed(body, b, i):
            before = BANKS[body][i][1]
            return use(body, b, 0) + MB_ if before is None else use(body, b, before) + 1 + MB_

        def unit_of(body, g, kind, k):
            return next(it[1] for it in BODIES[body][0][g] if it[2] == kind and it[5] == k) // HG + 1
        T_FIRST = FIRST.index(("T", 0, 0))

        assert (NU * HG) % SB_ == 0 and NU % EB == 0
        TENSORS = ((0, q_parts, 0), (2, k_parts, HD), (1, k_parts, 0), (3, q_parts, HD))
        PARTS_OUT = 12 * 16

        @block.sync
        def _(sp):
            sp.dma_start(X[:, 0:TB, :], x[0].rearrange("(t p) d -> p t d", p=P)).then_inc(x_in[0], 16)
            sp.dma_start(wm[:, :], wmod).then_inc(w_in, 16)
            for n, w in enumerate((Wq, Wk, Wv, Wo)):
                sp.dma_start(wraw[:, n, :], w).then_inc(w_in, 16)
            for b in range(1, B):
                sp.dma_start(X[:, b * TB:(b + 1) * TB, :], x[b].rearrange("(t p) d -> p t d", p=P)).then_inc(x_in[b], 16)
            sp.wait_ge(pool_chain, 1)
            for h in range(H):
                sp.dma_start(JB[h * HD:(h + 1) * HD, h * HD:(h + 1) * HD], J[h]).then_inc(j_in, 16)
            Q_ROWS = ((0, 0, 3), (3, 0, 2), (5, 0, 1))
            K_ROWS = ((0, 0, 1), (1, 0, 1), (2, 0, 1), (3, 1, 1), (4, 1, 1), (5, 2, 1))

            def load_group(b, g):
                for side, src, terms in ((0, q_parts, Q_ROWS), (1, k_parts, K_ROWS)):
                    for t, j, n in terms:
                        sp.dma_start(stacks[t * ROW:(t + n) * ROW, g, side, :, :],
                                     src[bass.ds(b, 1), g * HG:(g + 1) * HG, j:j + n, :, :].rearrange("a h j r q -> (a j r) h q"))\
                            .then_inc(stack_in[g], 16)
                sp.dma_start(Vs[:, g, :], VA[:, g, :, :, :].rearrange("p t h w -> p (t h w)"))\
                    .then_inc(stack_in[g], 16)

            def send_maxima(g, index):
                sp.wait_ge(max_used, index + 1 + MB_)
                for h in range(HG):
                    sp.dma_start(stacks[KROWS:MROWS, g, 0, h, :].rearrange("r (t q) -> r t q", t=TB),
                                 mrow[h * 3 * TB:(h + 1) * 3 * TB, :]).then_inc(m_in, 16)

            def store_half(b, g, half):
                sp.wait_ge(ot_ok, (b * NG + g) * 2 + half + 2)
                sp.dma_start(o_raw[bass.ds(b, 1), g, :, half * HALF:(half + 1) * HALF].rearrange("a p q -> (a p) q"),
                             OT[:, half, :]).then_inc(ot_out[half], 16)

            def prepared(b):
                sp.wait_ge(stored, b + 1)
                sp.sem_inc(sp_turn, 1)
                sp.wait_ge(va_ok, b + 1)
                sp.sem_inc(sp_turn, 1)

            for n, (k, dst, off) in enumerate(TENSORS):
                if n:
                    sp.wait_ge(split0_ok, n)
                else:
                    sp.wait_ge(split0_q, 1)
                for j in range(3):
                    sp.dma_start(dst[0, :, j, off:off + HD, :], T16[:, k, j, :]).then_inc(parts0_out, 16)
            prepared(0)
            for g in range(NG):
                load_group(0, g)
            send_maxima(0, T_FIRST)

            def by_head(b):
                return o_raw[bass.ds(b, 1), :, :, :].rearrange("a g (h r) q -> (a g h) r q", h=HG)

            def load_denominators(b):
                for half in range(2):
                    sp.wait_ge(ot_out[half], ((b + 1) * NG + 1) * 16)
                sp.dma_start(DENP[:, :], by_head(b)[:, HD, :].rearrange("k (t q) -> k t q", t=TB)).then_inc(den_in, 16)

            def store_reciprocals(b):
                sp.wait_ge(den_ok, b + 1)
                sp.dma_start(r_den[bass.ds(b, 1), :, :].rearrange("a h (t q) -> (a h t) q", t=TB), DENP[:, :]).then_inc(rden_out, 16)

            def load_outputs(b):
                sp.wait_ge(rden_out, (b + 1) * 16)
                sp.sem_inc(sp_turn, 1)
                if isinstance(b, int):
                    sp.wait_ge(stored, B)
                    sp.wait_ge(sent, b + 1)
                else:
                    sp.wait_ge(stored, b + 3)
                    sp.sem_inc(sp_turn, 1)
                sp.dma_start(NUM[:, :], by_head(b)[:, 0:HD, :]).then_inc(num_in, 16)
                sp.dma_start(DEN[:, :], r_den[bass.ds(b, 1), :, :].rearrange("a h (o q) -> (a h) o q", o=1).to_broadcast([H, HD, S]))\
                    .then_inc(num_in, 16)

            def attention(b, body):
                if body != "first":
                    load_denominators(b - 1)
                for g in range(NG):
                    store_half(b, g, 0)
                    if body != "last" or g + 1 < NG:
                        t_use = next(it[0] for it in BODIES[body][0][g] if it[2] == "T")
                        send_maxima((g + 1) % NG, use(body, b, t_use))
                    if g == 1 and body != "last":
                        prepared(b + 1)
                    if g == 1 and body != "first":
                        load_outputs(b - 1)
                    store_half(b, g, 1)
                    if g == 0 and body != "first":
                        store_reciprocals(b - 1)
                    if body != "last" and g:
                        for place in (0, 1) if g == 1 else (g,):
                            sp.wait_ge(pv_ok, (b * NG + place + 1) * NU + EB)
                            load_group(b + 1, place)
                    if body == "last" and g < 2:
                        sp.wait_ge(pv_ok, (b * NG + g + 1) * NU + EB)
                        if g == 0:
                            sp.dma_start(W1r, W1.rearrange("e (c f) d -> f (e c) d", f=P)).then_inc(w12_in, 16)
                        else:
                            sp.dma_start(W2r.rearrange("p (e c) f -> p e (c f)", e=E), W2.rearrange("e d n -> d e n"))\
                                .then_inc(w12_in, 16)
            attention(0, "first")
            with sp.Fori(1, B - 1) as b:
                attention(b, "middle")
            attention(B - 1, "last")
            load_denominators(B - 1)
            store_reciprocals(B - 1)
            load_outputs(B - 1)

            sp.wait_ge(pads_ok, 1)
            for e in range(E):
                first_row = sp.value_load(pad_slot[0:1, e:e + 1], min_val=0, max_val=E * REG - P)
                sp.dma_start(by_expert[bass.ds(first_row, P), :], pad_row[:, :]).then_inc(pads_out, 16)
            sp.wait_ge(pads_out, E * 16)
            sp.wait_ge(sorted_out, NT * 16)
            sp.wait_ge(tiles_ok, 1)

            def load_tile(n, j):
                first_row = sp.value_load(tile_row[0:1, bass.ds(n, 1)], min_val=0, max_val=E * REG - P)
                sp.dma_start(XS[:, j, :], by_expert[bass.ds(first_row, P), :]).then_inc(xs_in[j], 16)
            for j in range(U):
                load_tile(j, j)
            with sp.Fori(0, SLOT_TILES // U - 1) as i:
                for j in range(U):
                    sp.wait_ge(y_out[j % 2], (i * (U // 2) + j // 2 + 1) * 16)
                    sp.sem_inc(sp_turn, 1)
                    load_tile(i * U + U + j, j)

        @block.gpsimd
        def _(pool):
            g = nc.gpsimd
            g.memset(ident[:, :], 0.0)
            g.memset(mask[:, :], 0.0)
            g.memset(triu[:, :], 1.0)
            g.memset(onesb[:, :], 1.0)
            g.memset(after[:, :], 0.0)
            g.memset(JB[:, :], 0.0)
            g.iota(iotai[:, 0:SLOT_TILES], [[1, SLOT_TILES]], base=0, channel_multiplier=0)
            g.iota(iotai[:, 40:40 + NT + 1], [[P, NT + 1]], base=0, channel_multiplier=0)
            g.iota(iotai[:, 73:74], [[0, 1]], base=0, channel_multiplier=1)
            g.iota(token[:, :], [[P, NT]], base=0, channel_multiplier=1)
            g.memset(pad_row[:, 0:3 * D], 0.0)
            g.iota(pad_row[:, 3 * D:3 * D + 1].bitcast(I32), [[0, 1]], base=B * S, channel_multiplier=1).then_inc(pool_chain, 1)
            pool.wait_ge(pool_chain, 1)
            g.affine_select(out=ident[:, :], in_=ident[:, :], compare_op=ALU.not_equal, fill=1.0, base=0,
                            pattern=[[-1, P]], channel_multiplier=1)
            g.affine_select(out=mask[:, S - P:S], in_=mask[:, S - P:S], compare_op=ALU.is_ge, fill=-BIG, base=0,
                            pattern=[[-1, P]], channel_multiplier=1)
            g.affine_select(out=after[:, :], in_=after[:, :], compare_op=ALU.is_ge, fill=-BIG, base=0,
                            pattern=[[1, P]], channel_multiplier=-1)
            g.affine_select(out=triu[:, :], in_=triu[:, :], compare_op=ALU.is_gt, fill=0.0, base=0,
                            pattern=[[1, P]], channel_multiplier=-1).then_inc(pool_chain, 1)
            pool.wait_ge(pool_chain, 2)
            g.tensor_copy(iota_f[:, 0:74], iotai[:, 0:74])
            g.memset(VA.rearrange("p g t h w -> p (g t h) w")[:, :, HD:VW], 1.0).then_inc(pool_chain, 1)
            pool.wait_ge(pool_chain, 3)
            g.tensor_copy(identb[:, :], ident[:, :]).then_inc(consts_ok, 1)
            pool.wait_ge(consts_ok, 1)
            for r in range(NG):
                if r:
                    pool.wait_ge(ones_ok, r)
                g.memset(stacks[KROWS:MROWS, r, 1, :, :], 1.0).then_inc(ones_ok, 1)
            pool.wait_ge(ones_ok, NG)

            def split(b, n, done_sem):
                k = TENSORS[n][0]
                pool.wait_ge(first_ok, b * 4 + n + 1)
                a = T32[:, k, :]
                g.tensor_tensor(a, a, T16[:, k, 0, :], ALU.subtract).then_inc(split_step, 1)
                done = 2 * n if isinstance(b, int) and b == 0 else b * 8 - 6 + 2 * n
                pool.wait_ge(split_step, done + 1)
                g.tensor_tensor(T16[:, k, 1, :], a, mask[:, 0:1].to_broadcast([P, S]), ALU.add).then_inc(split_step, 1)
                pool.wait_ge(split_step, done + 2)
                g.tensor_tensor(T16[:, k, 2, :], a, T16[:, k, 1, :], ALU.subtract).then_inc(done_sem, 1)
            split(0, 0, split0_q)
            pool.wait_ge(parts0_out, PARTS_OUT)
            pool.sem_inc(stored, 1)

            def residual(b):
                pool.wait_ge(xn_ok, b + 1)
                pool.sem_inc(pool_turn, 1)
                xb = X[:, bass.ds(b * TB, TB), :]
                g.tensor_tensor(xb, xb, ga_bo[:, bass.ds(b, 1), :].to_broadcast([P, TB, D]), ALU.add).then_inc(res_ok, 1)

            def split_batch(b):
                for n, (k, dst, off) in enumerate(TENSORS):
                    split(b, n, split_ok)
                    pool.wait_ge(split_ok, b * 4 + n - 3)
                    pool.sem_inc(pool_turn, 1)
                    for j in range(3):
                        pool.dma_start(dst[bass.ds(b, 1), :, j, off:off + HD, :].rearrange("a h r q -> (a h) r q"),
                                       T16[:, k, j, :]).then_inc(parts_out, 16)
                residual(b)
                pool.wait_ge(parts_out, b * PARTS_OUT)
                pool.sem_inc(stored, 1)

            def send_rows(b):
                over = lambda k: MB[:, bass.ds(b, 1), k, :].to_broadcast([P, TB, D])
                pool.wait_ge(h2_ok, b + 1)
                pool.sem_inc(pool_turn, 1)
                g.tensor_tensor(PAY[:, :, D:2 * D], H2, over(3), ALU.mult).then_inc(pool_step, 1)
                pool.wait_ge(pool_step, b * 4 + 1)
                pool.sem_inc(pool_turn, 1)
                g.tensor_tensor(PAY[:, :, D:2 * D], PAY[:, :, D:2 * D], X[:, bass.ds(b * TB, TB), :], ALU.add).then_inc(pool_step, 1)
                g.tensor_tensor(PAYI[:, :, 3 * D], token[:, bass.ds(b * TB, TB)], iotai[:, 0:1].to_broadcast([P, TB]), ALU.add)\
                    .then_inc(pool_step, 1)
                pool.wait_ge(alpha_ok, b + 1)
                pool.sem_inc(pool_turn, 1)
                g.tensor_tensor(PAY[:, :, 2 * D:3 * D], rs[:, 2, :].unsqueeze(2).to_broadcast([P, TB, D]), over(3), ALU.mult)\
                    .then_inc(pool_step, 1)
                pool.wait_ge(pool_step, b * 4 + 4)
                pool.sem_inc(pool_turn, 1)
                pool.wait_ge(slots_ok, b + 1)
                pool.sem_inc(pool_turn, 1)
                pool.wait_ge(pay_ok, b + 1)
                pool.sem_inc(pool_turn, 1)
                for t in range(TB):
                    g.indirect_dma_start(by_expert, bass.IndirectOffsetOnAxis(ap=slot[:, t:t + 1], axis=0), PAY[:, t, :], None)\
                        .then_inc(sorted_out, 16)
                pool.wait_ge(sorted_out, (b + 1) * TB * 16)
                pool.sem_inc(sent, 1)
            pool.sem_inc(sent, 1)
            pool.wait_ge(mod_ok, 1)
            residual(0)
            split_batch(1)
            with pool.Fori(2, B) as b:
                split_batch(b)
                send_rows(b - 2)
            send_rows(B - 2)
            send_rows(B - 1)
            out_rows = out.rearrange("b s d -> (b s) d")
            with pool.Fori(0, SLOT_TILES // U) as i:
                for j in range(U):
                    pool.wait_ge(ys_ok, i * U + j + 1)
                    pool.sem_inc(pool_turn, 1)
                    g.indirect_dma_start(out_rows, bass.IndirectOffsetOnAxis(ap=XSI[:, j, 3 * D:3 * D + 1], axis=0), YS[:, j % 2, :],
                                         None, bounds_check=B * S - 1, oob_is_err=False).then_inc(y_out[j % 2], 16)
            for k in range(2):
                pool.wait_ge(y_out[k], SLOT_TILES // 2 * 16)

        @block.scalar
        def _(act):
            a = nc.scalar
            row = lambda v: v.rearrange("(a n) -> a n", a=1)
            for r0, src in ((0, b1.rearrange("e (c f) -> (e c) f", f=P)), (32, gamma), (40, beta), (48, cent), (56, c),
                            (60, row(bq)), (61, row(bk))):
                act.dma_start(rows[r0:r0 + src.shape[0], :], src).then_inc(rows_in, 16)
            act.dma_start(bv_b[:, :], row(bv).to_broadcast([P, D])).then_inc(bias_in, 16)
            act.dma_start(bo_b[:, :], row(bo).to_broadcast([P, D])).then_inc(bias_in, 16)
            act.dma_start(lam_c[:, :], row(lam).to_broadcast([P, 1])).then_inc(bias_in, 16)
            act.dma_start(b2_b[:, :], row(b2.rearrange("e d -> (e d)")).to_broadcast([P, E * D])).then_inc(bias_in, 16)
            act.wait_ge(cols_ok, 1)
            a.activation(silu[:, 0, :], cols[:, 56:60], ACT.Exp, scale=-1.0).then_inc(silu_e, 1)
            act.wait_ge(modT_ok, 1)
            act.sem_inc(exp_ok, SB_)
            act.sem_inc(ot_ok, 1)
            for half in range(2):
                act.sem_inc(ot_out[half], 16)

            def tanh_q(b):
                act.wait_ge(q32_ok, b + 1)
                if not (isinstance(b, int) and b == 0):
                    act.wait_ge(stored, b)
                if not isinstance(b, int):
                    act.wait_ge(sent, b - 1)
                a.activation(T32[:, 4, :], T32[:, 0, :], ACT.Tanh, scale=HD ** 0.5).then_inc(tanh_ok, 1)

            def first_q(b):
                a.activation(T16[:, 0, 0, :], T32[:, 0, :], ACT.Copy).then_inc(first_ok, 1)

            def tanh_k(b):
                act.wait_ge(k32_ok, b + 1)
                a.activation(T32[:, 2, :], T32[:, 1, :], ACT.Tanh)

            def first_tanh_k(b):
                a.activation(T16[:, 2, 0, :], T32[:, 1, :], ACT.Tanh).then_inc(first_ok, 1)

            def first_k(b):
                a.activation(T16[:, 1, 0, :], T32[:, 1, :], ACT.Copy).then_inc(first_ok, 1)

            def first_j(b):
                act.wait_ge(j32_ok, b + 1)
                a.activation(T16[:, 3, 0, :], T32[:, 3, :], ACT.Copy).then_inc(first_ok, 1)

            def sigmoid(b):
                act.wait_ge(best_ok, b + 1)
                a.activation(rs[:, 1, :], rs[:, 0, :], ACT.Tanh, scale=0.5).then_inc(alpha_t, 1)

            def act_steps(body):
                steps = {}
                if body != "last":
                    for k, which in ((3, (tanh_q, first_q)), (5, (tanh_k, first_tanh_k, first_k)), (9, (first_j,))):
                        for n, step in enumerate(which):
                            steps.setdefault((0, unit_of(body, 0, "P", k) + (n + 1) // 2), []).append((1 if n % 2 else 3, step, 1))
                if body != "first":
                    steps[3, min(NU - 1, unit_of(body, 3, "D", ("best", 0)))] = [(3, sigmoid, -1)]
                return steps
            for step in (tanh_q, first_q, tanh_k, first_tanh_k, first_k, first_j):
                step(0)

            def evacuate(b, g, half):
                act.wait_ge(pv_ok, (b * NG + g) * NU + max(u for u in HALF_END if HALF_END[u] == half) + 1 + EB)
                act.wait_ge(ot_out[half], (b * NG + g + 1) * 16)
                a.activation(OT[:, half, :], PS[:, 7, :], ACT.Copy).then_inc(ot_ok, 1)

            def attention(b, body):
                steps = act_steps(body)
                for g in range(NG):
                    for u, (qc, kb) in enumerate(UNITS):
                        off = max(0, kb - 4 * qc) * P
                        for h in range(HG):
                            n = u * HG + h
                            act.wait_ge(s_ps, (b * NG + g) * NU * HG + n + 1)
                            if h == 0:
                                act.wait_ge(pv_ok, (b * NG + g) * NU + u + 1)
                            a.activation(PT[:, u % EB, h, off:HALF], PS[:, 4 + n % SB_, off:HALF], ACT.Exp).then_inc(exp_ok, 1)
                            for at, step, ahead in steps.get((g, u), ()):
                                if at == h:
                                    step(b + ahead)
                        if u == LAG + 3:
                            evacuate(b, g, 0)
                        if u == LAG - 1 and g:
                            evacuate(b, g - 1, 1)
                evacuate(b, NG - 1, 1)
            attention(0, "first")
            with act.Fori(1, B - 1) as b:
                attention(b, "middle")
            attention(B - 1, "last")

            act.wait_ge(pv_ok, GROUPS * NU + EB)
            for k in range(16):
                act.wait_ge(w_tr, k + 1)
                dst = (W1T if k < 8 else W2T)[:, (k % 8) * HALF:(k % 8 + 1) * HALF]
                a.activation(dst, PS[:, 4 + k % 4, :], ACT.Copy).then_inc(w_ev, 1)
            sigmoid(B - 1)

            act.wait_ge(tiles_ok, 1)
            act.sem_inc(xt_ok, 2)
            act.sem_inc(hr_ok, 2)

            def turned(n, j):
                act.wait_ge(xsT_ps, n + 1)
                act.wait_ge(h_ps, n + 1)
                a.activation(XT[:, j % 2, :], PS[:, j % 2, 0:P], ACT.Copy).then_inc(xt_ok, 1)

            def hidden(n, j):
                act.wait_ge(h_ps, n + 1 + 2)
                act.wait_ge(y_ps, n + 1)
                for k in range(FC):
                    last = a.activation(HR[:, j % 2, k * P:(k + 1) * P], PS[:, 4 + j % 2, k * P:(k + 1) * P], ACT.Relu,
                                        bias=B1C[:, j % 4, k:k + 1])
                last.then_inc(hr_ok, 1)
            turned(0, 0)
            turned(1, 1)
            with act.Fori(0, SLOT_TILES // U - 1) as i:
                for j in range(U):
                    hidden(i * U + j, j)
                    turned(i * U + j + 2, j)
            for n in range(SLOT_TILES - U, SLOT_TILES):
                hidden(n, n)
                if n + 2 < SLOT_TILES:
                    turned(n + 2, n)

        @block.tensor
        def _(pe):
            t_ = nc.tensor
            mm = t_.matmul
            pe.sem_inc(pv_ok, EB)
            pe.wait_ge(consts_ok, 1)
            pe.wait_ge(rows_in, 7 * 16)
            t_.transpose(PS[:, 0, 0:62], rows[0:62, :], ident[0:62, 0:62]).then_inc(cols_ps, 1)
            pe.wait_ge(w_in, 5 * 16)
            for n in range(4):
                last = t_.transpose(PS[:, 1, n * P:(n + 1) * P], wraw[:, n, :], ident[:, :])
            last.then_inc(wT_ps, 1)
            pe.wait_ge(silu_ok, 1)
            for k in range(2):
                mm(PS[:, 2, k * B:(k + 1) * B], wm[:, k * D:(k + 1) * D], silu[:, 3, :], start=(k == 0), stop=True,
                   skip_group_check=True)
            for b in range(B):
                last = mm(PS[:, 4 + b, :], silu_b[:, b, :], wm[:, 2 * D:6 * D], start=True, stop=True)
            last.then_inc(mod_ps, 1)
            pe.wait_ge(wT_ok, 1)
            pe.wait_ge(modT_ok, 1)

            def project(b, step, bank):
                what, half = step[0], int(step[1])
                part = slice(half * HALF, (half + 1) * HALF)
                if what == "X":
                    if half == 0:
                        pe.wait_ge(xn_ok, b + 1)
                    for t in range(4):
                        last = t_.transpose(PS[:, bank, t * P:(t + 1) * P], XN[:, half * 4 + t, :], ident[:, :])
                elif what == "J":
                    if half == 0:
                        pe.wait_ge(tanh_ok, b + 1)
                    last = mm(PS[:, bank, :], JL[:, :], T32[:, 4, part], start=True, stop=True)
                elif what == "V":
                    for t in range(4):
                        n = half * 4 + t
                        last = mm(PS[:, bank, t * P:(t + 1) * P], HT[:, n * P:(n + 1) * P], wT[:, 2, :], start=(t == 0),
                                  stop=True, skip_group_check=True)
                else:
                    if step == "Q0":
                        pe.wait_ge(ht_ok, b + 1)
                    last = mm(PS[:, bank, :], wT[:, "QK".index(what), :], HT[:, part], start=True, stop=True)
                last.then_inc(max_ps, 1)

            def after_attention(b, step, bank):
                half = int(step[1]) if len(step) > 1 else 0
                if step[0] == "O":
                    if half == 0:
                        pe.wait_ge(at_ok, b + 1)
                    for t in range(4):
                        n = half * 4 + t
                        last = mm(PS[:, bank, t * P:(t + 1) * P], AT[:, n * P:(n + 1) * P],
                                  WOG[:, bass.ds(b, 1), :].rearrange("p a d -> p (a d)"), start=(t == 0), stop=True,
                                  skip_group_check=True)
                elif step[0] == "H":
                    if half == 0:
                        pe.wait_ge(h2_ok, b + 1)
                    for t in range(4):
                        last = t_.transpose(PS[:, bank, t * P:(t + 1) * P], H2[:, half * 4 + t, :], ident[:, :])
                elif step == "S":
                    pe.wait_ge(h2t_ok, b + 1)
                    for t in range(TB):
                        last = mm(PS[:, bank, t * E:(t + 1) * E], AT[:, t * P:(t + 1) * P], cols[:, 48:56], start=(t == 0),
                                  stop=True, skip_group_check=True)
                else:
                    pe.wait_ge(oh_ok, b + 1)
                    mm(PS[:, bank, 0:TB * E], triu[:, :], ohb[:, :], start=True, stop=True, skip_group_check=True)
                    for k in range(1, TB):
                        mm(PS[:, bank, k * E:TB * E], onesb[:, :], ohb[:, 0:(TB - k) * E], start=False, stop=True,
                           skip_group_check=True)
                    for t in range(TB):
                        last = mm(PS[:, bank + 1, 0:E], onesb[:, :], ohb[:, t * E:(t + 1) * E], start=(t == 0), stop=(t == TB - 1))
                last.then_inc(max_ps, 1)

            def maximum(kind, g, k, free, bank, loads, group):
                if free is not None:
                    pe.wait_ge(max_used, free)
                if kind == "P":
                    project(loads, PREP[k], bank)
                    return
                if kind == "R":
                    after_attention(loads, k, bank)
                    return
                if kind == "T":
                    pe.wait_ge(m_parts_ok, group + 1)
                    t_.transpose(PS[:, bank, 0:P // 2].bitcast(BF16)[0:HG * 3 * TB, :],
                                 mparts[:, :, :, :].rearrange("p h j t -> p (h j t)"), identb[:, :]).then_inc(max_ps, 1)
                    return
                h, t = MTILES[k]
                if k == 0:
                    pe.wait_ge(stack_in[g], (loads + 1) * 10 * 16)
                n = (t + 1) * P
                for c0 in range(0, n, HALF):
                    c1 = min(n, c0 + HALF)
                    last = mm(PS[:, bank + c0 // HALF, 0:c1 - c0], SQ(g, h)[0:KROWS, t * P:(t + 1) * P],
                              SK(g, h)[0:KROWS, c0:c1], start=True, stop=True)
                last.then_inc(max_ps, 1)

            for i, (kind, ahead, k) in enumerate(FIRST):
                bank, before = FIRST_BANKS[i]
                maximum(kind, ahead, k, None if before is None else before + 1 + MB_, bank, 0, ahead)

            def products(b, g, u):
                qc, kb = UNITS[u]
                pe.wait_ge(exp_ok, ((b * NG + g) * NU + u + 1) * HG + SB_)
                if kb == 0:
                    pe.wait_ge(ot_ok, (b * NG + g) * 2 + qc + 1)
                off = max(0, kb - 4 * qc) * P
                for h in range(HG):
                    last = mm(PS[32 * h:32 * h + VW, 7, off:HALF],
                              Vs[:, g, (kb * HG + h) * VW:(kb * HG + h + 1) * VW], PT[:, u % EB, h, off:HALF],
                              start=(kb == 0), stop=(u in HALF_END), skip_group_check=True)
                last.then_inc(pv_ok, 1)

            pe.wait_ge(ones_ok, NG)
            pe.wait_ge(mod_ok, 1)

            def attention(b, body):
                trail = []
                for g in range(NG):
                    gi = b * NG + g
                    todo = BODIES[body][0][g]
                    for u, (qc, kb) in enumerate(UNITS):
                        if u == 0:
                            pe.wait_ge(m_in, (gi + 1) * HG * 16)
                        off = max(0, kb - 4 * qc) * P
                        for h in range(HG):
                            n = u * HG + h
                            pe.wait_ge(exp_ok, gi * NU * HG + n + 1)
                            bank = PS[:, 4 + n % SB_, :]
                            last = mm(bank[:, off:HALF], SK(g, h)[0:MROWS, kb * P:(kb + 1) * P],
                                      SQ(g, h)[0:MROWS, qc * HALF + off:(qc + 1) * HALF], start=True, stop=True, skip_group_check=True)
                            if u in DIAG:
                                last = mm(bank[:, off:off + P], identb[:, :], after[:, :], start=False, stop=True,
                                          skip_group_check=True)
                            last.then_inc(s_ps, 1)
                            for i, _, kind, place, ahead, k in [it for it in todo if it[1] == n and it[2] != "D"]:
                                maximum(kind, place, k, freed(body, b, i), BANKS[body][i][0],
                                        b + {"P": 1, "R": -1}.get(kind, (g + ahead) // NG), gi + ahead)
                        trail.append((g, u))
                        if len(trail) > LAG:
                            products(b, *trail.pop(0))
                for g, u in trail:
                    products(b, g, u)
            attention(0, "first")
            with pe.Fori(1, B - 1) as b:
                attention(b, "middle")
            attention(B - 1, "last")

            def tail(k):
                bank, before = TAIL_BANKS[k]
                maximum("R", 0, POST[k], N_END + MB_ + (0 if before is None else before + 1), bank, B - 1, 0)
            pe.wait_ge(w12_in, 32)
            pe.wait_ge(exp_ok, GROUPS * NU * HG + SB_)
            pe.wait_ge(ot_ok, 2 * GROUPS + 1)
            for k in range(16):
                if k >= 4:
                    pe.wait_ge(w_ev, k - 3)
                for j in range(4):
                    n = (k % 8) * 4 + j
                    last = t_.transpose(PS[:, 4 + k % 4, j * P:(j + 1) * P], (W1r if k < 8 else W2r)[:, n, :], ident[:, :])
                last.then_inc(w_tr, 1)
            pe.wait_ge(w_ev, 16)
            for k, step in enumerate(POST):
                tail(k)
                if step == "O1":
                    for n in range(E * FC):
                        last = mm(PS[:, 4, n:n + 1], W1T[:, n * P:(n + 1) * P], cols[:, 40 + n // FC:41 + n // FC],
                                  start=(n == 0), stop=True, skip_group_check=True)
                    last.then_inc(b1_ps, 1)
            pe.wait_ge(tiles_ok, 1)
            pe.sem_inc(h_ps, 2)
            pe.sem_inc(y_ps, 2)

            def expert(n):
                return pe.value_load(tile_e[0:1, bass.ds(n, 1)], min_val=0, max_val=E - 1)

            def turn(n, j, q=None):
                pe.wait_ge(xs_in[j % U], ((n // U if q is None else q) + 1) * 16)
                pe.wait_ge(xt_ok, n + 1)
                t_.transpose(PS[:, j % 2, 0:P], XS[:, j % U, 0:D], ident[:, :]).then_inc(xsT_ps, 1)

            def up(n, j):
                pe.wait_ge(xt_ok, n + 1 + 2)
                pe.wait_ge(w1_ok, n + 1)
                pe.wait_ge(hr_ok, n + 1)
                for k in range(FC):
                    last = mm(PS[:, 4 + j % 2, k * P:(k + 1) * P], W1C[:, j % 2, k * P:(k + 1) * P], XT[:, j % 2, :],
                              start=(k == 0), stop=True, skip_group_check=True)
                last.then_inc(h_ps, 1)

            def down(n, j):
                e = expert(n)
                pe.wait_ge(hr_ok, n + 1 + 2)
                pe.wait_ge(ys_step, n * 2 + 1)
                for k in range(FC):
                    last = mm(PS[:, 6 + j % 2, 0:D], HR[:, j % 2, k * P:(k + 1) * P],
                              W2T[:, bass.ds(e * FF + k * P, P)], start=(k == 0), stop=(k == FC - 1))
                last.then_inc(y_ps, 1)

            def pe_step(n, j, h=True, tx=True, q=None):
                if tx:
                    turn(n + 2, j + 2, q)
                if h:
                    up(n + 1, j + 1)
                down(n, j)
            turn(0, 0)
            turn(1, 1)
            up(0, 0)
            with pe.Fori(0, SLOT_TILES // U - 1) as i:
                for j in range(U):
                    pe_step(i * U + j, j, q=i + (j + 2) // U)
            for n in range(SLOT_TILES - U, SLOT_TILES):
                pe_step(n, n, tx=n + 2 < SLOT_TILES, h=n + 1 < SLOT_TILES)

        @block.vector
        def _(dve):
            v = nc.vector
            count = [0]

            def link(ins):
                count[0] += 1
                ins.then_inc(dve_chain, 1)
                dve.wait_ge(dve_chain, count[0])

            def tt(o, a, b_, op):
                return v.tensor_tensor(o, a, b_, op)

            def moment_step(n, L, st):
                if n == 0:
                    tt(L(0), st[:, :, 1], st[:, :, 4], ALU.add)
                    tt(L(2), st[:, :, 2], st[:, :, 5], ALU.add)
                    return tt(L(1), st[:, :, 1], st[:, :, 4], ALU.subtract)
                if n == 1:
                    v.tensor_scalar(L(0), L(0), 0.5, None, ALU.mult)
                    return tt(L(3), L(1), L(1), ALU.mult)
                if n == 2:
                    return v.scalar_tensor_tensor(L(4), L(3), D / 4.0, L(2), ALU.mult, ALU.add)
                if n == 3:
                    return v.tensor_scalar(L(5), L(4), 1.0 / D, EPS, ALU.mult, ALU.add)
                if n == 4:
                    return v.tensor_scalar(L(6).bitcast(I32), L(5).bitcast(I32), 1, None, ALU.logical_shift_right)
                if n == 5:
                    return v.tensor_scalar(L(7).bitcast(I32), L(6).bitcast(I32), -1.0, float(0x5f3759df), ALU.mult, ALU.add)
                if n % 3 == 0:
                    return v.scalar_tensor_tensor(L(6), L(7), -0.5, L(7), ALU.mult, ALU.mult)
                if n % 3 == 1:
                    return tt(L(6), L(6), L(5), ALU.mult)
                return v.scalar_tensor_tensor(L(7), L(6), 1.5, L(7), ALU.add, ALU.mult)

            def normed(o, src, n):
                return v.tensor_scalar(o, src[:, bass.ds(n, 1), :].rearrange("p a d -> p (a d)"), lnt[:, 0, bass.ds(n, 1)],
                                       lnt[:, 7, bass.ds(n, 1)], ALU.subtract, ALU.mult)

            dve.sem_inc(max_used, MB_)
            dve.wait_ge(consts_ok, 1)
            v.tensor_scalar(base[:, :], iota_e, float(REG), None, ALU.mult)
            dve.wait_ge(cols_ps, 1)
            v.tensor_copy(cols[:, 0:62], PS[:, 0, 0:62]).then_inc(cols_ok, 1)
            dve.wait_ge(cols_ok, 1)
            v.tensor_scalar(bqs[:, :], cols[:, 60:61], HD ** -0.5, None, ALU.mult)
            dve.wait_ge(silu_e, 1)
            link(v.tensor_scalar(silu[:, 1, :], silu[:, 0, :], 1.0, None, ALU.add))
            link(v.reciprocal(silu[:, 2, :], silu[:, 1, :]))
            link(tt(silu[:, 3, :], silu[:, 2, :], cols[:, 56:60], ALU.mult))
            v.tensor_copy(silu_b[:, :, :], silu[:, 3, :].unsqueeze(2).to_broadcast([P, B, P])).then_inc(silu_ok, 1)
            dve.wait_ge(wT_ps, 1)
            v.tensor_copy(wT[:, :, :].rearrange("p n d -> p (n d)"), PS[:, 1, :]).then_inc(wT_ok, 1)
            def statistics(b0, b1, rounds):
                for b in range(b0, b1):
                    dve.wait_ge(x_in[b], 16)
                    for t in range(TB):
                        last = v.bn_stats(stat[:, b * TB + t, :], X[:, b * TB + t, :])
                last.then_inc(bn_ok, 1)
                dve.wait_ge(bn_ok, rounds)
                for n in range(MOMENTS):
                    link(moment_step(n, lambda k: lnt[:, k, b0 * TB:b1 * TB], stat[:, b0 * TB:b1 * TB, :]))
            statistics(0, 1, 1)
            dve.wait_ge(j_in, H * 16)
            dve.wait_ge(bias_in, 4 * 16)
            v.tensor_scalar(JL[:, :], JB[:, :], lam_c[:, :], None, ALU.mult)
            dve.wait_ge(mod_ps, 1)
            dve.wait_ge(wT_ok, 1)
            v.tensor_copy(modT[:, 0, :], PS[:, 2, 0:B])
            v.tensor_scalar(modT[:, 1, :], PS[:, 2, B:2 * B], 1.0, None, ALU.add).then_inc(modT_ok, 1)
            dve.wait_ge(modT_ok, 1)

            def conditioning():
                link(v.tensor_copy(MB[:, :, :, :].rearrange("p b k d -> p b (k d)"), PS[:, 4:8, :]))
                v.tensor_scalar(MB[:, :, 2, :], MB[:, :, 2, :], 1.0, None, ALU.add)
                for k in (0, 3):
                    gate, sign, size = MB[:, :, k, :], ga_bo[:, :, :], WOG[:, :, :]
                    link(v.tensor_scalar(sign, gate, 0.0, 2.0, ALU.is_ge, ALU.mult))
                    v.scalar_tensor_tensor(size, gate, -1.0, gate, ALU.mult, ALU.max)
                    link(v.tensor_scalar(sign, sign, 1.0, None, ALU.subtract))
                    link(v.scalar_tensor_tensor(gate, size, 0.25, sign, ALU.max, ALU.mult))
                tt(WOG[:, :, :], MB[:, :, 0, :], wT[:, 3:4, :].to_broadcast([P, B, D]), ALU.mult)
                tt(ga_bo[:, :, :], MB[:, :, 0, :], bo_b[:, :].unsqueeze(1).to_broadcast([P, B, D]), ALU.mult).then_inc(mod_ok, 1)
                dve.wait_ge(mod_ok, 1)

            def norm_row(b, t):
                if t == 0 and (not isinstance(b, int) or b):
                    dve.wait_ge(stored, b)
                if t == 0 and not isinstance(b, int):
                    dve.wait_ge(sent, b - 1)
                last = normed(XN[:, t, :], X, b * TB + t)
                if t == TB - 1:
                    last.then_inc(xn_ok, 1)

            def projected(b, step, bank):
                src = PS[:, bank, :]
                what, half = step[0], int(step[1])
                part = slice(half * HALF, (half + 1) * HALF)
                later = not isinstance(b, int) or b > 0
                if what == "X":
                    v.tensor_scalar(HT[:, part], src, modT[:, 1, bass.ds(b, 1)], modT[:, 0, bass.ds(b, 1)], ALU.mult, ALU.add)\
                        .then_inc(max_used, 1)
                elif what == "Q":
                    v.tensor_scalar(T32[:, 0, part], src, HD ** -0.5, bqs[:, :], ALU.mult, ALU.add).then_inc(max_used, 1)
                elif what == "K":
                    v.tensor_scalar(T32[:, 1, part], src, cols[:, 61:62], None, ALU.add).then_inc(max_used, 1)
                elif what == "J":
                    v.tensor_copy(T32[:, 3, part], src).then_inc(max_used, 1)
                else:
                    if later and half == 0:
                        for g in range(NG):
                            dve.wait_ge(stack_in[g], b * 10 * 16)
                    for g in range(NG):
                        last = tt(VA[:, g, half * 4:half * 4 + 4, :, 0:HD],
                                  src[:, 0:HALF].rearrange("p (t g h w) -> p g t h w", t=4, g=NG, h=HG)[:, g],
                                  bv_b[:, g * HG * HD:(g + 1) * HG * HD].rearrange("p (h w) -> p h w", h=HG).unsqueeze(1)
                                  .to_broadcast([P, 4, HG, HD]), ALU.add)
                    last.then_inc(max_used, 1)

            def linked(b, n):
                dve.wait_ge(post_chain, b * LINKS + n)
                dve.sem_inc(dve_turn, 1)

            def after_routing(b, n):
                dve.wait_ge(route_chain, b * ROUTE_LINKS + n)
                dve.sem_inc(dve_turn, 1)

            L2 = lambda k: ln2[:, k, :]
            over = lambda b, k: MB[:, bass.ds(b, 1), k, :].to_broadcast([P, TB, D])
            AT_X1, AT_ROOT_X = 0, 1
            AT_NORM_X = AT_ROOT_X + MOMENTS
            AT_SCALE, AT_STATS_H, AT_ROOT_H = AT_NORM_X + 1, AT_NORM_X + 2, AT_NORM_X + 3
            AT_NORM_H = LINKS = AT_ROOT_H + MOMENTS
            RANK, PLACE, ROUTE_LINKS = 4, 5, 7

            def half_stats(src, half):
                for t in range(half * 4, half * 4 + 4):
                    last = v.bn_stats(stat2[:, t, :], src(t))
                if half:
                    last.then_inc(post_chain, 1)

            def half_norm(b, dst, src, half):
                for t in range(half * 4, half * 4 + 4):
                    last = v.tensor_scalar(dst(t), src(t), ln2[:, 0, t:t + 1], ln2[:, 7, t:t + 1], ALU.subtract, ALU.mult)
                return last

            x_tile = lambda b: lambda t: X[:, bass.ds(b * TB + t, 1), :].rearrange("p a d -> p (a d)")
            h_tile = lambda t: H2[:, t, :]
            row_tile = lambda t: PAY[:, t, 0:D]

            def only_dve(b, step):
                if step == "denominators":
                    dve.wait_ge(den_in, (b + 1) * 16)
                    dve.sem_inc(dve_turn, 1)
                    v.reciprocal(DENP[:, :], DENP[:, :]).then_inc(den_ok, 1)
                elif step == "attended":
                    dve.wait_ge(num_in, (b + 1) * 2 * 16)
                    tt(AT[:, :], NUM[:, :], DEN[:, :], ALU.mult).then_inc(at_ok, 1)
                elif step in ("stats_x0", "stats_x1"):
                    half_stats(x_tile(b), int(step[-1]))
                elif step in ("norm_x0", "norm_x1"):
                    linked(b, AT_NORM_X)
                    last = half_norm(b, h_tile, x_tile(b), int(step[-1]))
                    if step[-1] == "1":
                        last.then_inc(post_chain, 1)
                elif step == "scale_h":
                    linked(b, AT_SCALE)
                    tt(H2, H2, over(b, 2), ALU.mult).then_inc(post_chain, 1)
                elif step == "shift_h":
                    linked(b, AT_SCALE + 1)
                    tt(H2, H2, over(b, 1), ALU.add).then_inc(h2_ok, 1)
                elif step in ("stats_h0", "stats_h1"):
                    dve.wait_ge(h2_ok, b + 1)
                    dve.sem_inc(dve_turn, 1)
                    half_stats(h_tile, int(step[-1]))
                elif step in ("norm_h0", "norm_h1"):
                    linked(b, AT_NORM_H)
                    last = half_norm(b, row_tile, h_tile, int(step[-1]))
                    if step[-1] == "1":
                        last.then_inc(pay_ok, 1)
                elif step[0] in ("root_x", "root_h"):
                    n = (AT_ROOT_X if step[0] == "root_x" else AT_ROOT_H) + step[1]
                    linked(b, n)
                    moment_step(step[1], L2, stat2).then_inc(post_chain, 1)
                elif step[0] == "best":
                    best(b, step[1])
                elif step[0] == "place":
                    place_rows(b, step[1])
                elif step == "place":
                    place_rows(b)
                else:
                    assert step == "weigh"
                    dve.wait_ge(alpha_t, b + 1)
                    v.tensor_scalar(rs[:, 2, :], rs[:, 1, :], 0.5, 0.5, ALU.mult, ALU.add).then_inc(alpha_ok, 1)

            flat = lambda r: r.rearrange("p t d -> p (t d)")
            sc, cand, onehot, rank = (rt[:, k, :, :] for k in range(4))
            col = lambda r: r.unsqueeze(2).to_broadcast([P, TB, E])

            def best(b, n):
                if n == 0:
                    v.tensor_reduce(rs[:, 0, :], sc, AX.X, ALU.max).then_inc(best_ok, 1)
                    return
                if n == 1:
                    dve.wait_ge(best_ok, b + 1)
                    dve.sem_inc(dve_turn, 1)
                    last = tt(cand, sc, col(rs[:, 0, :]), ALU.is_ge)
                else:
                    after_routing(b, n - 1)
                if n == 2:
                    last = v.scalar_tensor_tensor(cand, cand, -float(E), iota_e.unsqueeze(1).to_broadcast([P, TB, E]), ALU.mult, ALU.add)
                elif n == 3:
                    last = v.tensor_reduce(rs[:, 3, :], cand, AX.X, ALU.min)
                elif n == 4:
                    last = tt(onehot, cand, col(rs[:, 3, :]), ALU.is_equal)
                if n == 5:
                    v.tensor_copy(ohb[:, :], flat(onehot)).then_inc(oh_ok, 1)
                else:
                    last.then_inc(route_chain, 1)

            def place_rows(b, n):
                if n == 0:
                    after_routing(b, RANK + 1)
                    tt(rank, rank, onehot, ALU.mult).then_inc(route_chain, 1)
                    return
                after_routing(b, PLACE + n)
                if n == 1:
                    v.tensor_reduce(rs[:, 3, :], rank, AX.X, ALU.add).then_inc(route_chain, 1)
                else:
                    v.tensor_copy(slot[:, :], rs[:, 3, :]).then_inc(slots_ok, 1)

            def reduced(b, step, bank):
                half = int(step[1]) if len(step) > 1 else 0
                if step[0] == "O":
                    if half == 0:
                        dve.wait_ge(res_ok, b + 1)
                        dve.sem_inc(dve_turn, 1)
                    rows_ = flat(X[:, bass.ds(b * TB + half * 4, 4), :])
                    tt(rows_, rows_, PS[:, bank, :], ALU.add).then_inc(max_used, 1)
                elif step[0] == "H":
                    v.tensor_copy(AT[:, half * HALF:(half + 1) * HALF], PS[:, bank, :]).then_inc(max_used, 1)
                elif step == "S":
                    v.tensor_copy(flat(sc), PS[:, bank, 0:TB * E]).then_inc(max_used, 1)
                else:
                    tt(rank, PS[:, bank, 0:TB * E].rearrange("p (t e) -> p t e", e=E),
                       base[:, :].unsqueeze(1).to_broadcast([P, TB, E]), ALU.add)
                    tt(few[:, :], PS[:, bank + 1, 0:E], base[:, :], ALU.add).then_inc(route_chain, 1)
                    after_routing(b, RANK + 1)
                    v.tensor_copy(base[:, :], few[:, :]).then_inc(max_used, 1)

            def maximum(kind, place, k, index, bank, group):
                if kind == "D":
                    only_dve(group, k)
                    return
                dve.wait_ge(max_ps, index + 1)
                if kind == "R":
                    reduced(group, k, bank)
                    dve.wait_ge(max_used, index + 1 + MB_)
                    dve.sem_inc(h2t_ok if k == "H1" else dve_turn, 1)
                    return
                if kind == "P":
                    projected(group, PREP[k], bank)
                    signal = dict(X1=ht_ok, Q1=q32_ok, K1=k32_ok, J1=j32_ok, V1=va_ok).get(PREP[k])
                    if signal is not None:
                        dve.wait_ge(max_used, index + 1 + MB_)
                        dve.sem_inc(signal, 1)
                    return
                if kind == "T":
                    if not (isinstance(group, int) and group == 0):
                        dve.wait_ge(m_in, group * HG * 16)
                    v.tensor_copy(mrow[:, :], PS[:, bank, 0:P // 2].bitcast(BF16)[0:HG * 3 * TB, :]).then_inc(max_used, 1)
                    return
                h, t = MTILES[k]
                n = (t + 1) * P
                src = PS[:, bank:bank + (n + HALF - 1) // HALF, :].rearrange("p a q -> p (a q)")[:, 0:n]
                dve.sem_inc(dve_turn, 1)
                v.tensor_tensor_reduce(out=src, in0=src, in1=mask[:, S - n:S], scale=1.0, scalar=-3e38, op0=ALU.add, op1=ALU.max,
                                       accum_out=maxima[:, place, h * TB + t:h * TB + t + 1]).then_inc(max_used, 1)
                if k == NM - 1:
                    m = maxima[:, place, :].rearrange("p (h t) -> p h t", h=HG)
                    rest = mres[:, 0, :].rearrange("p (h t) -> p h t", h=HG)
                    dve.wait_ge(max_used, index + 1 + MB_)
                    for step, ins in enumerate((
                            lambda: v.tensor_scalar(mparts[:, :, 0, :], m, -1.0, None, ALU.mult),
                            lambda: v.scalar_tensor_tensor(rest, m, -1.0, mparts[:, :, 0, :], ALU.mult, ALU.subtract),
                            lambda: v.tensor_copy(mparts[:, :, 1, :], rest))):
                        ins().then_inc(m_split, 1)
                        dve.wait_ge(m_split, group * 3 + step + 1)
                    tt(mparts[:, :, 2, :], rest, mparts[:, :, 1, :], ALU.subtract).then_inc(m_parts_ok, 1)

            for t in range(TB):
                norm_row(0, t)
            def split0(n):
                k = TENSORS[n][0]
                dve.wait_ge(first_ok, n + 1)
                a = T32[:, k, :]
                steps = 2 * (n - 1)
                tt(a, a, T16[:, k, 0, :], ALU.subtract).then_inc(split0_step, 1)
                dve.wait_ge(split0_step, steps + 1)
                v.tensor_copy(T16[:, k, 1, :], a).then_inc(split0_step, 1)
                dve.wait_ge(split0_step, steps + 2)
                tt(T16[:, k, 2, :], a, T16[:, k, 1, :], ALU.subtract).then_inc(split0_ok, 1)

            for i, (kind, ahead, k) in enumerate(FIRST):
                maximum(kind, ahead, k, i, FIRST_BANKS[i][0], ahead)
                if i == len(PREP) - 1:
                    for n in range(1, 4):
                        split0(n)
                    conditioning()
                    statistics(1, B, 2)

            def attention(b, body):
                for g in range(NG):
                    for n, (i, _, kind, place, ahead, k) in enumerate(BODIES[body][0][g]):
                        maximum(kind, place, k, use(body, b, i), BANKS[body][i][0] if kind != "D" else None,
                                b + 1 if kind == "P" else b - 1 if kind in "RD" else b * NG + g + ahead)
                        if g == 0 and n < TB and body != "last":
                            norm_row(b + 1, n)
            attention(0, "first")
            with dve.Fori(1, B - 1) as b:
                attention(b, "middle")
            attention(B - 1, "last")

            only_dve(B - 1, "denominators")
            only_dve(B - 1, "attended")
            k = 0
            for g in (2, 3):
                for _, kind, step in POST_AT[g]:
                    if kind == "R":
                        maximum("R", 0, step, N_END + k, TAIL_BANKS[k][0], B - 1)
                        k += 1
                    elif step != "attended":
                        only_dve(B - 1, step)
            dve.wait_ge(slots_ok, B)
            v.tensor_copy(pad_slot[:, :], base[:, :]).then_inc(pads_ok, 1)
            many, total, region, step_row = (ts[:, k, 0:E] for k in range(4))
            link(v.scalar_tensor_tensor(many, iota_e, -float(REG), base[:, :], ALU.mult, ALU.add))
            link(tt(tw, many.unsqueeze(2).to_broadcast([P, E, NT + 1]), iota_n.unsqueeze(1).to_broadcast([P, E, NT + 1]), ALU.is_gt))
            link(v.tensor_reduce(many, tw, AX.X, ALU.add))
            link(v.memset(ts[:, 4, :], 1.0))
            link(v.tensor_tensor_scan(total, ts[:, 4, 0:E], many, 0.0, ALU.mult, ALU.add))
            link(tt(region, total, many, ALU.subtract))
            link(v.tensor_scalar(region, region, -float(P), None, ALU.mult))
            link(v.scalar_tensor_tensor(region, iota_e, float(REG), region, ALU.mult, ALU.add))
            link(tt(step_row[:, 0:E - 1], region[:, 1:E], region[:, 0:E - 1], ALU.subtract))
            link(tt(tv, total[:, 0:E - 1].unsqueeze(1).to_broadcast([P, SLOT_TILES, E - 1]),
                    iota_t.unsqueeze(2).to_broadcast([P, SLOT_TILES, E - 1]), ALU.is_le))
            link(tt(tu, tv, step_row[:, 0:E - 1].unsqueeze(1).to_broadcast([P, SLOT_TILES, E - 1]), ALU.mult))
            link(v.tensor_reduce(ts[:, 4, :], tv, AX.X, ALU.add))
            v.tensor_copy(tile_e[:, :], ts[:, 4, :])
            link(v.tensor_reduce(ts[:, 3, :], tu, AX.X, ALU.add))
            link(v.scalar_tensor_tensor(ts[:, 3, :], iota_t, float(P), ts[:, 3, :], ALU.mult, ALU.add))
            link(v.tensor_scalar(ts[:, 3, :], ts[:, 3, :], region[:, 0:1], None, ALU.add))
            link(v.tensor_scalar(ts[:, 3, :], ts[:, 3, :], base[:, E - 1:E], None, ALU.min))
            dve.wait_ge(b1_ps, 1)
            tt(b1p[:, :], PS[:, 4, 0:E * FC], cols[:, 0:E * FC], ALU.add)
            v.tensor_copy(tile_row[:, :], ts[:, 3, :]).then_inc(tiles_ok, 1)

            dve.wait_ge(tiles_ok, 1)
            dve.sem_inc(ys_step, 4)
            known = {}

            def expert(n, key):
                if key not in known:
                    known[key] = dve.value_load(tile_e[0:1, bass.ds(n, 1)], min_val=0, max_val=E - 1)
                return known[key]

            def copy_w1(n, j):
                e = expert(n, j)
                dve.wait_ge(h_ps, n + 1)
                v.tensor_copy(B1C[:, j % 4, :], b1p[:, bass.ds(e * FC, FC)])
                v.tensor_scalar(W1C[:, j % 2, :], W1T[:, bass.ds(e * FF, FF)], cols[:, bass.ds(e + 32, 1)], None, ALU.mult)\
                    .then_inc(w1_ok, 1)

            def finished(n, j, q):
                e = expert(n, j)
                dve.wait_ge(y_ps, n + 1 + 2)
                if q is not None:
                    dve.wait_ge(y_out[j % 2], q * 16)
                y = YS[:, j % 2, :]
                tt(y, PS[:, 6 + j % 2, 0:D], b2_b[:, bass.ds(e * D, D)], ALU.add).then_inc(ys_step, 1)
                dve.wait_ge(ys_step, n * 2 + 5)
                tt(y, y, XS[:, j % U, 2 * D:3 * D], ALU.mult).then_inc(ys_step, 1)
                dve.wait_ge(ys_step, n * 2 + 6)
                tt(y, y, XS[:, j % U, D:2 * D], ALU.add).then_inc(ys_ok, 1)
            copy_w1(0, 0)
            copy_w1(1, 1)
            known.clear()
            for n in range(U):
                copy_w1(n + 2, n + 2)
                finished(n, n, n // 2 if n >= 2 else None)
            with dve.Fori(1, SLOT_TILES // U - 1) as i:
                known.clear()
                for j in range(U):
                    copy_w1(i * U + j + 2, j + 2)
                    finished(i * U + j, j, i * (U // 2) + j // 2)
            known.clear()
            for n in range(SLOT_TILES - U, SLOT_TILES):
                if n + 2 < SLOT_TILES:
                    copy_w1(n + 2, n + 2)
                finished(n, n, n // 2)


_INS = ['L0_attn_x', 'L0_attn_Wq', 'L0_attn_bq', 'L0_attn_Wk', 'L0_attn_bk', 'L0_attn_Wv', 'L0_attn_bv', 'L0_attn_Wo',
        'L0_attn_bo', 'L0_attn_J_attn', 'L0_attn_lambda_attn', 'L0_ffn_centroids', 'L0_ffn_gamma', 'L0_ffn_beta',
        'L0_ffn_W1', 'L0_ffn_b1', 'L0_ffn_W2', 'L0_ffn_b2', 'L0_c', 'L0_wmod']
_OUTS = [((B, S, D), 'float32')]


def kernel(**inputs):
    import numpy as _np
    import concourse.bacc as _bacc
    from concourse import mybir as _mybir
    from concourse.bass_utils import run_bass_kernel_spmd as _run

    nc = _bacc.Bacc("TRN2", target_bir_lowering=False, num_devices=1)
    arrays, args = {}, []
    for name in _INS:
        a = _np.ascontiguousarray(inputs[name])
        if a.ndim == 0:
            a = a.reshape(1)
        arrays[f"in_{name}_dram"] = a
        args.append(nc.dram_tensor(f"in_{name}_dram", a.shape, _mybir.dt.from_np(a.dtype), kind="ExternalInput").ap())
    for i, (shape, dtype) in enumerate(_OUTS):
        dt = _mybir.dt.from_np(_np.dtype(dtype))
        args.append(nc.dram_tensor(f"out_{i}_dram", shape, dt, kind="ExternalOutput").ap())
    build(nc, *args)
    r = _run(nc, [arrays], core_ids=[0])
    got = tuple(r.results[0][f"out_{i}_dram"] for i in range(len(_OUTS)))
    return got[0]
```
